# Optimizing a Trainium2 kernel written in Bass

```python
import numpy as np
import jax
import jax.numpy as jnp

def _softmax(x, axis=-1):
    return jax.nn.softmax(x, axis=axis)

def _gelu(x):
    return jax.nn.gelu(x, approximate=True)

def _silu(x):
    return jax.nn.silu(x)

def _sigmoid(x):
    return jax.nn.sigmoid(x)

def _layernorm(x, axis=-1, eps=1e-05):
    m = jnp.mean(x, axis=axis, keepdims=True)
    v = jnp.var(x, axis=axis, keepdims=True)
    return (x - m) / jnp.sqrt(v + eps)

def _scatter_add(tgt, idx, src, axis=0):
    return tgt.at[idx].add(src)

def _segment_sum(src, seg, n):
    return jax.ops.segment_sum(src, seg, n)
kernel_name = 'mk_conv_seq_d2_conv_nchw256_r4_4a30dc'

def setup_inputs(seed: int=0):
    np.random.seed(seed)
    _w = jnp.asarray

    def _rec_inputs():
        import jax
        import jax.numpy as jnp
        _gk = jax.random.key(seed)
        x = -0.000125 + 0.9999 * jax.random.normal(jax.random.fold_in(_gk, 1), (8, 64, 32, 32), jnp.float32)
        return x
    x = _rec_inputs()

    def _L0_conv_setup():
        import jax, jax.numpy as jnp
        import numpy as np
        WS = 8
        HEADS = 8
        EPS = 1e-05

        def _rel_pos_index(ws):
            coords = np.stack(np.meshgrid(np.arange(ws), np.arange(ws), indexing='ij')).reshape(2, -1)
            rel = coords[:, :, None] - coords[:, None, :]
            rel = rel.transpose(1, 2, 0).astype(np.int64)
            rel[..., 0] += ws - 1
            rel[..., 1] += ws - 1
            rel[..., 0] *= 2 * ws - 1
            return jnp.asarray(rel.sum(-1))
        REL_IDX = _rel_pos_index(WS)

        def _layernorm(x, scale, bias):
            mu = jnp.mean(x, axis=-1, keepdims=True)
            var = jnp.mean(jnp.square(x - mu), axis=-1, keepdims=True)
            return (x - mu) * jax.lax.rsqrt(var + EPS) * scale + bias

        def _window_attention(xw, w_qkv, b_qkv, w_proj, b_proj, rel_bias_table):
            Bn, N, C = xw.shape
            d = C // HEADS
            scale = d ** (-0.5)
            qkv = xw @ w_qkv + b_qkv
            qkv = qkv.reshape(Bn, N, 3, HEADS, d)
            q, k, v = (qkv[:, :, 0], qkv[:, :, 1], qkv[:, :, 2])
            attn = jnp.einsum('bnhd,bmhd->bhnm', q * scale, k)
            bias = rel_bias_table[REL_IDX.reshape(-1)].reshape(N, N, HEADS)
            attn = attn + bias.transpose(2, 0, 1)[None]
            attn = jax.nn.softmax(attn, axis=-1)
            out = jnp.einsum('bhnm,bmhd->bnhd', attn, v).reshape(Bn, N, C)
            return out @ w_proj + b_proj
        key = jax.random.key(seed)
        ks = jax.random.split(key, 8)
        B, C, H, W = (8, 64, 32, 32)
        hid = 4 * C
        nb = (2 * WS - 1) ** 2
        return {'x': jax.random.normal(ks[0], (B, C, H, W), jnp.float32), 'ln1_scale': jnp.ones((C,), jnp.float32), 'ln1_bias': jnp.zeros((C,), jnp.float32), 'w_qkv': jax.random.normal(ks[1], (C, 3 * C), jnp.float32) * 0.02, 'b_qkv': jnp.zeros((3 * C,), jnp.float32), 'w_proj': jax.random.normal(ks[2], (C, C), jnp.float32) * 0.02, 'b_proj': jnp.zeros((C,), jnp.float32), 'rel_bias_table': jax.random.normal(ks[3], (nb, HEADS), jnp.float32) * 0.02, 'ln2_scale': jnp.ones((C,), jnp.float32), 'ln2_bias': jnp.zeros((C,), jnp.float32), 'w_mlp1': jax.random.normal(ks[4], (C, hid), jnp.float32) * 0.02, 'b_mlp1': jnp.zeros((hid,), jnp.float32), 'w_mlp2': jax.random.normal(ks[5], (hid, C), jnp.float32) * 0.02, 'b_mlp2': jnp.zeros((C,), jnp.float32)}
    _L0_conv_all = _L0_conv_setup()
    _L0_conv_in = {k: v for k, v in _L0_conv_all.items() if k in ('ln1_scale', 'ln1_bias', 'w_qkv', 'b_qkv', 'w_proj', 'b_proj', 'rel_bias_table', 'ln2_scale', 'ln2_bias', 'w_mlp1', 'b_mlp1', 'w_mlp2', 'b_mlp2')}
    del _L0_conv_all

    def _L1_conv_setup():
        import jax, jax.numpy as jnp
        import numpy as np

        def _dw_conv(x, w, ks):
            pad = (ks - 1) // 2
            return jax.lax.conv_general_dilated(x, w, window_strides=(1, 1), padding=[(pad, pad), (pad, pad)], feature_group_count=x.shape[1], dimension_numbers=('NCHW', 'OIHW', 'NCHW'))
        key = jax.random.key(seed)
        ks = jax.random.split(key, 12)
        B, Cin, M, O, H, W = (8, 64, 64, 64, 32, 32)
        k = 32
        inp = {'x': jax.random.normal(ks[0], (B, Cin, H, W), jnp.float32), 'pw1_w': jax.random.normal(ks[1], (M, Cin), jnp.float32) * 0.02, 'pw1_b': jnp.zeros((M,), jnp.float32), 'fc1_w': jax.random.normal(ks[2], (2 * M, M), jnp.float32) * 0.02, 'fc1_b': jnp.zeros((2 * M,), jnp.float32), 'fc2_w': jax.random.normal(ks[3], (M, 2 * M), jnp.float32) * 0.02, 'fc2_b': jnp.zeros((M,), jnp.float32), 'off_w': jax.random.normal(ks[4], (6, M), jnp.float32) * 0.02, 'off_b': jnp.zeros((6,), jnp.float32), 'dw3': jax.random.normal(ks[5], (M, 1, 3, 3), jnp.float32) * 0.1, 'dw5': jax.random.normal(ks[6], (M, 1, 5, 5), jnp.float32) * 0.1, 'dw7': jax.random.normal(ks[7], (M, 1, 7, 7), jnp.float32) * 0.1, 'pw_w': jax.random.normal(ks[8], (O, 3 * M), jnp.float32) * 0.02, 'pw_b': jnp.zeros((O,), jnp.float32), 'k': k}
        return inp
    _L1_conv_all = _L1_conv_setup()
    _L1_conv_in = {k: v for k, v in _L1_conv_all.items() if k in ('pw1_w', 'pw1_b', 'fc1_w', 'fc1_b', 'fc2_w', 'fc2_b', 'off_w', 'off_b', 'dw3', 'dw5', 'dw7', 'pw_w', 'pw_b')}
    del _L1_conv_all
    return {'x': x, 'L0_conv_ln1_scale': _L0_conv_in['ln1_scale'], 'L0_conv_ln1_bias': _L0_conv_in['ln1_bias'], 'L0_conv_w_qkv': _L0_conv_in['w_qkv'], 'L0_conv_b_qkv': _L0_conv_in['b_qkv'], 'L0_conv_w_proj': _L0_conv_in['w_proj'], 'L0_conv_b_proj': _L0_conv_in['b_proj'], 'L0_conv_rel_bias_table': _L0_conv_in['rel_bias_table'], 'L0_conv_ln2_scale': _L0_conv_in['ln2_scale'], 'L0_conv_ln2_bias': _L0_conv_in['ln2_bias'], 'L0_conv_w_mlp1': _L0_conv_in['w_mlp1'], 'L0_conv_b_mlp1': _L0_conv_in['b_mlp1'], 'L0_conv_w_mlp2': _L0_conv_in['w_mlp2'], 'L0_conv_b_mlp2': _L0_conv_in['b_mlp2'], 'L1_conv_pw1_w': _L1_conv_in['pw1_w'], 'L1_conv_pw1_b': _L1_conv_in['pw1_b'], 'L1_conv_fc1_w': _L1_conv_in['fc1_w'], 'L1_conv_fc1_b': _L1_conv_in['fc1_b'], 'L1_conv_fc2_w': _L1_conv_in['fc2_w'], 'L1_conv_fc2_b': _L1_conv_in['fc2_b'], 'L1_conv_off_w': _L1_conv_in['off_w'], 'L1_conv_off_b': _L1_conv_in['off_b'], 'L1_conv_dw3': _L1_conv_in['dw3'], 'L1_conv_dw5': _L1_conv_in['dw5'], 'L1_conv_dw7': _L1_conv_in['dw7'], 'L1_conv_pw_w': _L1_conv_in['pw_w'], 'L1_conv_pw_b': _L1_conv_in['pw_b']}

def reference(x, L0_conv_ln1_scale, L0_conv_ln1_bias, L0_conv_w_qkv, L0_conv_b_qkv, L0_conv_w_proj, L0_conv_b_proj, L0_conv_rel_bias_table, L0_conv_ln2_scale, L0_conv_ln2_bias, L0_conv_w_mlp1, L0_conv_b_mlp1, L0_conv_w_mlp2, L0_conv_b_mlp2, L1_conv_pw1_w, L1_conv_pw1_b, L1_conv_fc1_w, L1_conv_fc1_b, L1_conv_fc2_w, L1_conv_fc2_b, L1_conv_off_w, L1_conv_off_b, L1_conv_dw3, L1_conv_dw5, L1_conv_dw7, L1_conv_pw_w, L1_conv_pw_b):
    import jax
    import jax.numpy as jnp

    def _L0_conv_ref(x, ln1_scale, ln1_bias, w_qkv, b_qkv, w_proj, b_proj, rel_bias_table, ln2_scale, ln2_bias, w_mlp1, b_mlp1, w_mlp2, b_mlp2):
        import jax, jax.numpy as jnp
        import numpy as np
        WS = 8
        HEADS = 8
        EPS = 1e-05

        def _rel_pos_index(ws):
            coords = np.stack(np.meshgrid(np.arange(ws), np.arange(ws), indexing='ij')).reshape(2, -1)
            rel = coords[:, :, None] - coords[:, None, :]
            rel = rel.transpose(1, 2, 0).astype(np.int64)
            rel[..., 0] += ws - 1
            rel[..., 1] += ws - 1
            rel[..., 0] *= 2 * ws - 1
            return jnp.asarray(rel.sum(-1))
        REL_IDX = _rel_pos_index(WS)

        def _layernorm(x, scale, bias):
            mu = jnp.mean(x, axis=-1, keepdims=True)
            var = jnp.mean(jnp.square(x - mu), axis=-1, keepdims=True)
            return (x - mu) * jax.lax.rsqrt(var + EPS) * scale + bias

        def _window_attention(xw, w_qkv, b_qkv, w_proj, b_proj, rel_bias_table):
            Bn, N, C = xw.shape
            d = C // HEADS
            scale = d ** (-0.5)
            qkv = xw @ w_qkv + b_qkv
            qkv = qkv.reshape(Bn, N, 3, HEADS, d)
            q, k, v = (qkv[:, :, 0], qkv[:, :, 1], qkv[:, :, 2])
            attn = jnp.einsum('bnhd,bmhd->bhnm', q * scale, k)
            bias = rel_bias_table[REL_IDX.reshape(-1)].reshape(N, N, HEADS)
            attn = attn + bias.transpose(2, 0, 1)[None]
            attn = jax.nn.softmax(attn, axis=-1)
            out = jnp.einsum('bhnm,bmhd->bnhd', attn, v).reshape(Bn, N, C)
            return out @ w_proj + b_proj
        B, C, H, W = x.shape
        xc = jnp.transpose(x, (0, 2, 3, 1))
        xn = _layernorm(xc, ln1_scale, ln1_bias)
        nh, nw = (H // WS, W // WS)
        win = xn.reshape(B, nh, WS, nw, WS, C).transpose(0, 1, 3, 2, 4, 5)
        win = win.reshape(B * nh * nw, WS * WS, C)
        aw = _window_attention(win, w_qkv, b_qkv, w_proj, b_proj, rel_bias_table)
        x_attn = aw.reshape(B, nh, nw, WS, WS, C).transpose(0, 1, 3, 2, 4, 5).reshape(B, H, W, C)
        xc = xc + x_attn
        h = _layernorm(xc, ln2_scale, ln2_bias)
        h = jax.nn.gelu(h @ w_mlp1 + b_mlp1, approximate=False) @ w_mlp2 + b_mlp2
        xc = xc + h
        return jnp.transpose(xc, (0, 3, 1, 2))

    def _L1_conv_ref(x, pw1_w, pw1_b, fc1_w, fc1_b, fc2_w, fc2_b, off_w, off_b, dw3, dw5, dw7, pw_w, pw_b, k):
        import jax, jax.numpy as jnp
        import numpy as np

        def _dw_conv(x, w, ks):
            pad = (ks - 1) // 2
            return jax.lax.conv_general_dilated(x, w, window_strides=(1, 1), padding=[(pad, pad), (pad, pad)], feature_group_count=x.shape[1], dimension_numbers=('NCHW', 'OIHW', 'NCHW'))
        B, _, H, W = x.shape
        residual = x
        h = jnp.einsum('bchw,oc->bohw', x, pw1_w) + pw1_b[None, :, None, None]
        gap = h.mean(axis=(2, 3))
        hid = jax.nn.relu(gap @ fc1_w.T + fc1_b)
        scores = jax.nn.sigmoid(hid @ fc2_w.T + fc2_b)
        _, idx = jax.lax.top_k(scores, k)
        mask = jnp.zeros_like(scores).at[jnp.arange(B)[:, None], idx].set(1.0)
        h = jax.nn.relu(h)
        gap2 = h.mean(axis=(2, 3))
        offsets = jnp.tanh(gap2 @ off_w.T + off_b).reshape(B, 3, 2)
        sel = (h * mask[:, :, None, None])[:, :k]
        conv_in = sel.reshape(1, B * k, H, W)
        outs = []
        for i, (ksz, base) in enumerate([(3, dw3), (5, dw5), (7, dw7)]):
            scale = jax.nn.sigmoid(offsets[:, i, 0]).reshape(B, 1, 1, 1, 1)
            shift = jnp.tanh(offsets[:, i, 1]).reshape(B, 1, 1, 1, 1)
            w = base[:k][None] * (1.0 + scale) + shift
            y = _dw_conv(conv_in, w.reshape(B * k, 1, ksz, ksz), ksz)
            outs.append(y.reshape(B, k, H, W))
        fused = jnp.concatenate(outs, axis=1)
        sel_pw = pw_w[:, :3 * k]
        out = jnp.einsum('bchw,oc->bohw', fused, sel_pw) + pw_b[None, :, None, None]
        return out + residual

    def _gn(v, G=32, eps=1e-05):
        B_, C_, H_, W_ = v.shape
        g = v.reshape(B_, G, C_ // G, H_, W_)
        m = jnp.mean(g, axis=(2, 3, 4), keepdims=True)
        s = jnp.var(g, axis=(2, 3, 4), keepdims=True)
        return ((g - m) / jnp.sqrt(s + eps)).reshape(v.shape)

    def _ln_c(v, eps=1e-06):
        m = jnp.mean(v, axis=1, keepdims=True)
        s = jnp.var(v, axis=1, keepdims=True)
        return (v - m) / jnp.sqrt(s + eps)

    def _ln_t(v, eps=1e-05):
        m = jnp.mean(v, axis=-1, keepdims=True)
        s = jnp.var(v, axis=-1, keepdims=True)
        return (v - m) / jnp.sqrt(s + eps)

    def _to_tokens(v):
        B_, C_, H_, W_ = v.shape
        return v.reshape(B_, C_, H_ * W_).transpose(0, 2, 1)

    def _from_tokens(t, like):
        B_, C_, H_, W_ = like.shape
        return t.transpose(0, 2, 1).reshape(B_, C_, H_, W_)
    x = _L0_conv_ref(x, L0_conv_ln1_scale, L0_conv_ln1_bias, L0_conv_w_qkv, L0_conv_b_qkv, L0_conv_w_proj, L0_conv_b_proj, L0_conv_rel_bias_table, L0_conv_ln2_scale, L0_conv_ln2_bias, L0_conv_w_mlp1, L0_conv_b_mlp1, L0_conv_w_mlp2, L0_conv_b_mlp2)
    x = _L1_conv_ref(x, L1_conv_pw1_w, L1_conv_pw1_b, L1_conv_fc1_w, L1_conv_fc1_b, L1_conv_fc2_w, L1_conv_fc2_b, L1_conv_off_w, L1_conv_off_b, L1_conv_dw3, L1_conv_dw5, L1_conv_dw7, L1_conv_pw_w, L1_conv_pw_b, 32)
    return x

_drawn_inputs = setup_inputs


def setup_inputs(seed=0):
    import zlib

    import numpy as np

    out = dict(_drawn_inputs(seed))
    spreads = {'L0_conv_ln1_scale': (1.0, 0.6),
     'L0_conv_ln1_bias': (0.0, 0.8),
     'L0_conv_b_qkv': (0.0, 0.435),
     'L0_conv_b_proj': (0.0, 0.1),
     'L0_conv_ln2_scale': (1.0, 0.6),
     'L0_conv_ln2_bias': (0.0, 2.0),
     'L0_conv_b_mlp1': (0.0, 0.432),
     'L0_conv_b_mlp2': (0.0, 0.1),
     'L1_conv_pw1_b': (0.0, 0.599),
     'L1_conv_fc1_b': (0.0, 0.8),
     'L1_conv_fc2_b': (0.0, 0.339),
     'L1_conv_off_b': (0.0, 0.362),
     'L1_conv_pw_b': (0.0, 0.1)}
    factors = {'L0_conv_w_qkv': 8.0,
     'L0_conv_w_proj': 3.004,
     'L0_conv_rel_bias_table': 8.0,
     'L1_conv_pw1_w': 4.899,
     'L1_conv_fc2_w': 5.633,
     'L1_conv_off_w': 8.0,
     'L1_conv_dw3': 8.0,
     'L1_conv_dw5': 8.0,
     'L1_conv_dw7': 5.522}
    for name, (base, spread) in spreads.items():
        noise = np.random.default_rng([zlib.crc32(name.encode()), seed]).standard_normal(out[name].shape)
        drawn = base * np.exp(spread * noise) if base else spread * noise
        out[name] = jnp.asarray(drawn.astype(out[name].dtype))
    for name, factor in factors.items():
        out[name] = (out[name] * factor).astype(out[name].dtype)
    return out
```

```python
import numpy as np
import concourse.bass as bass
from concourse import mybir
from contextlib import ExitStack

B, C, H, W = 8, 64, 32, 32
WS, NH, HD = 8, 8, 8
NB4 = B // 2
PIX = H * W
COLS = NB4 * PIX
G = 512
NG = COLS // G
NW = G // (WS * WS)
T = WS * WS
HIDDEN = 4 * C
KS = C // 2
KERNELS = (3, 5, 7)
TAP = 7
PAD = TAP // 2
PATCH = WS * (2 * WS - 1)
PW = W + 2 * PAD
PIMG = PW * (H + 2 * PAD)
PBUF = PIMG + 4
NKT = 2 * TAP
EPS1 = 1e-5
SCALE = float(HD) ** -0.5

_p = np.arange(128)
_bh, _c = _p // C, _p % C


def _valid():
    v = np.zeros((128, len(KERNELS), TAP, 2), np.float32)
    for i, k in enumerate(KERNELS):
        o = (TAP - k) // 2
        for p in range(128):
            for half in range(2):
                dx = 4 * half + p // KS
                if o <= dx < TAP - o:
                    v[p, i, o:TAP - o, half] = 1
    return v.reshape(128, -1)


_CONST = {
    "center": np.where(_bh[:, None] == _bh, (_p[:, None] == _p) - 1.0 / C, 0),
    "average": np.where(_bh[:, None] == _bh, 1.0 / C, 0),
    "ident": _p[:, None] == _p,
    "reverse": (_p % T)[:, None] == T - 1 - _p % T,
    "head_of_channel": (_c // HD)[:, None] == np.arange(NH),
    "head_of_row": (_p % NH)[:, None] == np.arange(NH),
    "window_of_row": (_p // NH % NW)[:, None] == np.arange(NW),
    "same_half": _bh[:, None] == _bh,
    "ones_by_head_half": (np.arange(64) // 32 == np.arange(64) % 32 // 16)[None]
    & (_bh[:, None] == np.arange(64) % 16 // HD),
    "earlier": np.arange(C) < (_p % KS)[:, None],
    "valid": _valid(),
    "batch_of_row": _p[:, None] == np.arange(B),
}
_AT, _n = {}, 0
for _k, _v in _CONST.items():
    _AT[_k] = (_n, _n + _v.shape[1])
    _n += _v.shape[1]
NCONST = _n
NFIRST = _AT["average"][1]


def _constants():
    return np.ascontiguousarray(np.concatenate([np.asarray(v, np.float32) for v in _CONST.values()], axis=1))


def conv_seq_kernel(nc, d, out):
    F32, F32R = mybir.dt.float32, mybir.dt.float32r
    ALU, ACT, AX = mybir.AluOpType, mybir.ActivationFunctionType, mybir.AxisListType

    ctx = ExitStack()
    with ctx:
        def sb(name, shape, dt=F32):
            return ctx.enter_context(nc.sbuf_tensor(name, shape, dt))

        def sem(name):
            return ctx.enter_context(nc.semaphore(name))

        consts = sb("consts", [128, NCONST])

        def const(name):
            a, b = _AT[name]
            return consts[:, a:b]

        x = sb("x", [128, COLS])
        x1 = sb("x1", [128, COLS])
        x2 = x
        normed2 = sb("normed2", [128, COLS])
        proj_w = sb("proj_w", [128, 128])
        mlp2_w = sb("mlp2_w", [128, 2, C])
        pw1_w = sb("pw1_w", [128, 128])
        fc1_w = sb("fc1_w", [128, 2 * C])
        fc2_w = sb("fc2_w", [128, C])
        off_w = sb("off_w", [128, 6])
        fuse_w = sb("fuse_w", [128, 3, C])
        taps = sb("taps", [128, 3, NKT])
        vec = sb("vec", [128, 16])
        fc2_bias = sb("fc2_bias", [B, C])
        off_bias = sb("off_bias", [128, 6])
        qkv_w = sb("qkv_w", [128, 3, 128])
        mlp1_w = sb("mlp1_w", [128, 2, HIDDEN])
        qkv_bias = sb("qkv_bias", [128, 3])
        q_bias = sb("q_bias", [128, 1])
        proj_bias = sb("proj_bias", [128, 1])
        mlp1_bias = sb("mlp1_bias", [128, 2])
        eps = sb("eps", [128, 1])
        rel_raw = x1[0:T, 0:2 * NH * PATCH].rearrange("p (n h f) -> p n h f", n=2, h=NH)
        rel = sb("rel", [128, 2, NH * T], F32R)
        reverse = sb("reverse", [128, 128], F32R)
        pick = sb("pick", [128, NW, 128], F32R)
        square_logvar = sb("square_logvar", [128, 2, G])
        square, logvar = square_logvar[:, 0, :], square_logvar[:, 1, :]
        rstd = sb("rstd", [128, G])
        normed = sb("normed", [128, G])
        q = sb("q", [128, G])
        k = sb("k", [128, G])
        q_blocks = sb("q_blocks", [128, NW, 128], F32R)
        k_heads = sb("k_heads", [128, NW, NH, T], F32R)
        arena = sb("arena", [128, 18 * 1024])
        a0 = [0]

        def carve(*shape):
            n = int(np.prod(shape))
            a0[0] += n
            names = " ".join("abcdef"[:len(shape)])
            return arena[:, a0[0] - n:a0[0]].rearrange(f"p ({names}) -> p {names}", **dict(zip("abcdef", shape)))

        q_heads = carve(2, NW, NH, T)
        k_blocks = carve(2, NW, 128)
        probs = carve(NW, NH * T)
        v_blocks = carve(2, NW * NH * 32)
        a0[0] = 10 * 1024
        qkv_raw = carve(3, 128)
        proj_raw = carve(128)
        mlp1_raw = carve(2, HIDDEN)
        a0[0] = 0
        shifted = carve(2, 2, PIMG)
        conv_w = carve(2, 2, NKT, C)
        conv_t = carve(NKT, C)
        gap2_rep = carve(B, 128)
        greater, equal = carve(B, C), carve(B, C)
        score_diag = carve(B, C)[0:B]
        score_rep = carve(4, KS)[0:B]
        live = carve(B, NKT)
        tap_w = carve(3, B, NKT)
        score_row = carve(C)[0:B]
        offset = carve(B, 6)
        gain = carve(B, 6)
        shift = carve(B, 6)
        fc1_out = carve(B)
        score_col = carve(B)
        rank = carve(B)
        a0[0] = 14 * 1024
        hidden = carve(2, 4, G)
        maxima = sb("maxima", [128, NW * NH])
        maxima_t = sb("maxima_t", [128, T])
        minus_max = sb("minus_max", [128, NH, T], F32R)
        inv_sum = sb("inv_sum", [128, 4 * T])
        attended = sb("attended", [128, G])
        projected = sb("projected", [128, G])
        square_logvar2 = sb("square_logvar2", [128, 2, G])
        square2, logvar2 = square_logvar2[:, 0, :], square_logvar2[:, 1, :]
        mlp_out, result = square_logvar, square_logvar2
        rstd2 = sb("rstd2", [128, G])
        act_img = sb("act_img", [128, NB4, PBUF])
        h_sum = sb("h_sum", [128, NG])
        r_sum = sb("r_sum", [128, NG])
        pooled = sb("pooled", [128, 2, NB4])
        gap = sb("gap", [128, B])
        gap2 = sb("gap2", [128, B])
        ones8 = sb("ones8", [B, 128])

        psum = ctx.enter_context(nc.psum_tensor("psum", [128, 8, 512], F32))
        NORM, MISC0, MISC1, MAX0, PROB0, PV = 0, 1, 2, 3, 5, 7

        S = {n: sem(n) for n in (
            "zeroed", "consts_in", "x_first", "x_rest", "weights_in", "rel_in", "setup_dve", "setup_pe", "ready",
            "pe_xc", "pe_var", "pe_q", "pe_k", "pe_v", "pe_max", "pe_maxt", "pe_scores", "pe_pv", "pe_proj", "pe_xc2", "pe_var2",
            "ac_sq", "ac_log", "ac_rstd", "ac_q", "ac_k", "ac_v", "ac_probs", "ac_proj", "ac_sq2", "ac_log2", "ac_rstd2",
            "dv_normed", "dv_qb", "dv_kh", "dv_kb", "dv_qh", "dv_max", "dv_maxt", "dv_minus", "dv_inv", "dv_att", "dv_x1", "dv_normed2",
            "pe_mlp1", "pe_mlp2", "pe_pw1", "ac_gelu", "ac_mlp", "ac_relu", "dv_x2", "dv_hsum", "dv_rsum",
            "gate_dve", "gate_pe", "gate_act", "dv_convw", "dv_mulw", "shift_in0", "shift_in1", "pe_conv", "dv_result", "out_done0", "out_done1")}

        w_in = d["w_qkv"].rearrange("c (i o) -> c i o", i=3)
        loads = []
        for bh in range(2):
            r = slice(bh * C, (bh + 1) * C)
            loads += [(qkv_raw[r, :, bh * C:(bh + 1) * C], w_in),
                      (vec[r, 0:1], d["ln1_scale"]), (vec[r, 1:2], d["ln1_bias"])]
        first_loads = len(loads)
        for bh in range(2):
            r = slice(bh * C, (bh + 1) * C)
            loads += [(proj_raw[r, bh * C:(bh + 1) * C], d["w_proj"]),
                      (mlp1_raw[r, bh, :], d["w_mlp1"]),
                      (pw1_w[r, bh * C:(bh + 1) * C], d["pw1_t"]),
                      (fc1_w[r, :], d["fc1_t"]), (off_w[r, :], d["off_t"]),
                      (vec[r, 2:3], d["ln2_scale"]), (vec[r, 3:4], d["ln2_bias"]),
                      (vec[r, 4:7], d["b_qkv"]), (vec[r, 7:8], d["b_proj"]), (vec[r, 8:9], d["b_mlp2"]),
                      (vec[r, 9:10], d["pw1_b"]), (vec[r, 10:11], d["pw_b"])]
            for j in range(4):
                for hh in range(2):
                    row, head = j * 32 + hh * 16 + bh * HD, 4 * hh + j
                    loads.append((proj_w[row:row + HD, bh * C:(bh + 1) * C], d["w_proj"][head * HD:(head + 1) * HD, :]))
        loads += [(vec[:, 11:13], d["b_mlp1"]), (vec[:, 13:14], d["fc1_b"]),
                  (mlp2_w[:, :, :], d["w_mlp2"].rearrange("(f p) c -> p f c", p=128)),
                  (fc2_w[:, :], d["fc2_t"]), (taps[:, :, :], d["taps"]),
                  (fc2_bias[:, :], d["fc2_b"].partition_broadcast(B)),
                  (off_bias[:, :], d["off_b"].partition_broadcast(128))]
        for r in range(4):
            loads.append((fuse_w[r * KS:(r + 1) * KS, :, :], d["fuse_t"].rearrange("(i c) o -> c i o", i=3)))

        rel_loads = []
        side = 2 * WS - 1
        run = (WS - 1) * side + WS
        for n, name in enumerate(("rel_flipped", "rel_table")):
            for r in range(WS):
                src = bass.AP(d[name].tensor, d[name].offset + r * side, [[1, WS], [side * side, NH], [1, run]])
                rel_loads.append((rel_raw[r * WS:(r + 1) * WS, n, :, 0:run], src))

        def x_view(g, s):
            base = g * G + s * (G // 2)
            return x[:, bass.ds(base, G // 2)].rearrange("p (a w b) -> p w a b", a=WS, b=WS)

        def stripe(t, s):
            return t[:, s * (G // 2):(s + 1) * (G // 2)].rearrange("p (w a b) -> p w a b", a=WS, b=WS)

        block = ctx.enter_context(nc.Block())

        @block.sync
        def _(sp):
            sp.dma_start(consts[:, 0:NFIRST], d["consts"][:, 0:NFIRST]).then_inc(S["consts_in"], 16)
            for b4 in range(NB4):
                for bh in range(2):
                    sp.dma_start(x[bh * C:(bh + 1) * C, b4 * PIX:(b4 + 1) * PIX],
                                 d["x"][bh * NB4 + b4, :, :]).then_inc(S["x_rest" if b4 else "x_first"], 16)
                if b4 == 0:
                    sp.dma_start(consts[:, NFIRST:], d["consts"][:, NFIRST:]).then_inc(S["consts_in"], 16)
                    for dst, src in rel_loads:
                        sp.dma_start(dst, src).then_inc(S["rel_in"], 16)

            def copy_images(b4, par):
                for bh in range(2):
                    for r in range(4):
                        sp.dma_start(shifted[r * KS:(r + 1) * KS, par, bh, :],
                                     act_img[bh * C:bh * C + KS, b4, r:r + PIMG]).then_inc(S[f"shift_in{par}"], 16)

            sp.wait_ge(S["ac_relu"], NG)
            copy_images(0, 0)
            copy_images(1, 1)
            for b4 in range(NB4):
                for half in range(2):
                    n = 2 * b4 + half
                    sp.wait_ge(S["dv_result"], n + 1)
                    for bh in range(2):
                        sp.dma_start(out[bh * NB4 + b4, :, half * G:(half + 1) * G],
                                     result[bh * C:(bh + 1) * C, n % 2, :]).then_inc(S[f"out_done{half}"], 16)
                if b4 + 2 < NB4:
                    sp.wait_ge(S["pe_conv"], 2 * (b4 + 1))
                    copy_images(b4 + 2, b4 % 2)
            for half in range(2):
                sp.wait_ge(S[f"out_done{half}"], 32 * NB4)

        @block.gpsimd
        def _(pool):
            pool.memset(qkv_raw, 0.0).then_inc(S["zeroed"], 1)
            for t in (proj_raw, proj_w[:], mlp1_raw, pw1_w[:]):
                pool.memset(t, 0.0).then_inc(S["zeroed"], 1)
            pool.memset(q_blocks[:].bitcast(F32), 0.0).then_inc(S["zeroed"], 1)
            pool.memset(ones8[:], 1.0).then_inc(S["zeroed"], 1)
            for t in (v_blocks, k_blocks, gap[:], gap2[:], act_img[:]):
                pool.memset(t, 0.0).then_inc(S["zeroed"], 1)
        NZERO = 12

        @block.scalar
        def _(act):
            act.wait_ge(S["zeroed"], 1)
            for dst, src in loads[:first_loads]:
                act.dma_start(dst, src).then_inc(S["weights_in"], 16)
            act.wait_ge(S["zeroed"], 5)
            for dst, src in loads[first_loads:]:
                act.dma_start(dst, src).then_inc(S["weights_in"], 16)

            def square_of_centered(n):
                act.wait_ge(S["pe_xc"], n + 1)
                act.activation(square, psum[:, NORM, :], ACT.Square).then_inc(S["ac_sq"], 1)

            def inverse_deviation(n):
                act.wait_ge(S["pe_var"], n + 1)
                act.activation(logvar, psum[:, MISC0, :], ACT.Ln, bias=eps[:, 0:1]).then_inc(S["ac_log"], 1)
                act.wait_ge(S["ac_log"], n + 1)
                act.activation(rstd[:], logvar, ACT.Exp, scale=-0.5).then_inc(S["ac_rstd"], 1)

            def evacuate_qkv(n, par):
                act.wait_ge(S["pe_q"], n + 1)
                act.activation(q[:], psum[:, MISC0, :], ACT.Identity, bias=q_bias[:, 0:1], scale=SCALE).then_inc(S["ac_q"], 1)
                act.wait_ge(S["pe_k"], n + 1)
                act.activation(k[:], psum[:, MISC1, :], ACT.Identity, bias=qkv_bias[:, 1:2]).then_inc(S["ac_k"], 1)
                act.wait_ge(S["pe_v"], n + 1)
                vb = v_blocks[:, par, :].rearrange("p (w two h e) -> p w two h e", two=2, h=NH, e=32)
                vp = psum[:, MAX0 + 1, :].rearrange("p (w b h e) -> p w b h e", b=2, h=NH, e=HD)
                for odd in range(2):
                    for bh in range(2):
                        act.copy(vb[bh * C:(bh + 1) * C, :, odd, :, bh * HD:(bh + 1) * HD],
                                 vp[odd * T:(odd + 1) * T, :, bh, :, :]).then_inc(S["ac_v"], 1)

            def exponentials(g, w):
                act.wait_ge(S["pe_scores"], NW * g + w + 1)
                act.activation(probs[:, w, :], psum[:, PROB0 + w % 2, :], ACT.Exp).then_inc(S["ac_probs"], 1)

            def evacuate_projection(c):
                act.wait_ge(S["pe_proj"], c + 1)
                act.activation(projected[:], psum[:, MISC1, :], ACT.Identity, bias=proj_bias[:, 0:1]).then_inc(S["ac_proj"], 1)

            def square_of_centered2(c):
                act.wait_ge(S["pe_xc2"], c + 1)
                act.activation(square2, psum[:, NORM, :], ACT.Square).then_inc(S["ac_sq2"], 1)

            def inverse_deviation2(c):
                act.wait_ge(S["pe_var2"], c + 1)
                act.activation(logvar2, psum[:, MISC1, :], ACT.Ln, bias=eps[:, 0:1]).then_inc(S["ac_log2"], 1)
                act.wait_ge(S["ac_log2"], c + 1)
                act.activation(rstd2[:], logvar2, ACT.Exp, scale=-0.5).then_inc(S["ac_rstd2"], 1)

            def step(g, nxt, prev, par):
                if nxt is not None:
                    square_of_centered(nxt)
                exponentials(g, 0)
                exponentials(g, 1)
                if nxt is not None:
                    inverse_deviation(nxt)
                exponentials(g, 2)
                if prev is not None:
                    evacuate_projection(prev)
                exponentials(g, 3)
                if nxt is not None:
                    evacuate_qkv(nxt, 1 - par)
                exponentials(g, 4)
                if prev is not None:
                    square_of_centered2(prev)
                exponentials(g, 5)
                if prev is not None:
                    inverse_deviation2(prev)
                exponentials(g, 6)
                exponentials(g, 7)

            act.wait_ge(S["ready"], 1)
            square_of_centered(0)
            inverse_deviation(0)
            act.wait_ge(S["zeroed"], 9)
            evacuate_qkv(0, 0)
            step(0, 1, None, 0)
            with act.Fori(0, NG // 2 - 1) as i:
                step(2 * i + 1, 2 * i + 2, 2 * i, 1)
                step(2 * i + 2, 2 * i + 3, 2 * i + 1, 0)
            step(NG - 1, None, NG - 2, 1)
            evacuate_projection(NG - 1)
            square_of_centered2(NG - 1)
            inverse_deviation2(NG - 1)

            def gelu(n, par):
                for m in range(4):
                    act.wait_ge(S["pe_mlp1"], 4 * n + m + 1)
                    act.activation(hidden[:, par, m, :], psum[:, m, :], ACT.Gelu, bias=mlp1_bias[:, m % 2:m % 2 + 1]).then_inc(S["ac_gelu"], 1)

            def evacuate_mlp(n, par):
                act.wait_ge(S["pe_mlp2"], n + 1)
                act.activation(mlp_out[:, par, :], psum[:, 4 + par, :], ACT.Identity, bias=vec[:, 8:9]).then_inc(S["ac_mlp"], 1)

            def relu(n, b4, half):
                act.wait_ge(S["pe_pw1"], n + 1)
                img = act_img[:, b4, 0:PIMG].rearrange("p (y x) -> p y x", x=PW)
                act.activation(img[:, PAD + half * 16:PAD + half * 16 + 16, PAD:PAD + W],
                               psum[:, 6 + half, :].rearrange("p (y x) -> p y x", x=W), ACT.Relu, bias=vec[:, 9:10]).then_inc(S["ac_relu"], 1)

            act.wait_ge(S["zeroed"], NZERO)
            gelu(0, 0)
            gelu(1, 1)
            evacuate_mlp(0, 0)
            with act.Fori(0, NG // 2 - 1) as i:
                gelu(2 * i + 2, 0)
                evacuate_mlp(2 * i + 1, 1)
                relu(2 * i, i, 0)
                gelu(2 * i + 3, 1)
                evacuate_mlp(2 * i + 2, 0)
                relu(2 * i + 1, i, 1)
            evacuate_mlp(NG - 1, 1)
            relu(NG - 2, NB4 - 1, 0)
            relu(NG - 1, NB4 - 1, 1)

            act.wait_ge(S["gate_dve"], 4)
            act.activation(score_row, score_row, ACT.Sigmoid).then_inc(S["gate_act"], 1)
            act.wait_ge(S["gate_dve"], 5)
            act.activation(offset, offset, ACT.Tanh).then_inc(S["gate_act"], 1)
            act.wait_ge(S["gate_act"], 2)
            act.activation(gain, offset, ACT.Sigmoid).then_inc(S["gate_act"], 1)
            act.activation(shift, offset, ACT.Tanh).then_inc(S["gate_act"], 1)

        @block.tensor
        def _(pe):
            def centered(n):
                if isinstance(n, int) and n < 3:
                    pass
                else:
                    pe.wait_ge(S["dv_normed2"], n - 2)
                for s in range(2):
                    ins = pe.matmul(psum[:, NORM, s * 256:(s + 1) * 256], const("center"), x_view(n, s), start=True, stop=True)
                ins.then_inc(S["pe_xc"], 1)

            def variance(n, first=False):
                pe.wait_ge(S["ac_sq"], n + 1)
                if not first:
                    pe.wait_ge(S["dv_maxt"], n)
                pe.matmul(psum[:, MISC0, :], const("average"), square, start=True, stop=True).then_inc(S["pe_var"], 1)

            def qkv(n, first=False, second=False):
                pe.wait_ge(S["dv_normed"], n + 1)
                pe.matmul(psum[:, MISC0, :], qkv_w[:, 0, :], normed[:], start=True, stop=True).then_inc(S["pe_q"], 1)
                if not (first or second):
                    pe.wait_ge(S["ac_proj"], n - 1)
                pe.matmul(psum[:, MISC1, :], qkv_w[:, 1, :], normed[:], start=True, stop=True).then_inc(S["pe_k"], 1)
                if not first:
                    pe.wait_ge(S["dv_max"], NW * n)
                for m in range(4):
                    ins = pe.matmul(psum[:, MAX0 + 1, m * 128:(m + 1) * 128], normed[:, m * 128:(m + 1) * 128],
                                    qkv_w[:, 2, :], start=True, stop=True)
                ins.then_inc(S["pe_v"], 1)

            def scores_for_max(n, w):
                if w == 0:
                    pe.wait_ge(S["dv_qb"], n + 1)
                    pe.wait_ge(S["dv_kh"], n + 1)
                if w == 1:
                    pe.wait_ge(S["ac_v"], 4 * (n + 1))
                if w >= 2:
                    pe.wait_ge(S["dv_max"], NW * n + w - 1)
                pe.matmul(psum[:, MAX0 + w % 2, :], q_blocks[:, w, :], k_heads[:, w, :, :], start=True, stop=False)
                pe.matmul(psum[:, MAX0 + w % 2, :], reverse[:], rel[:, 0, :], start=False, stop=True).then_inc(S["pe_max"], 1)

            def transpose_maxima(n):
                pe.wait_ge(S["dv_max"], NW * (n + 1))
                pe.wait_ge(S["ac_q"], n + 1)
                pe.matmul(psum[0:C, MISC0, 0:128], maxima[:], const("ident"), start=True, stop=True).then_inc(S["pe_maxt"], 1)

            def scores(g, w, par):
                if w == 0:
                    pe.wait_ge(S["dv_kb"], g + 1)
                    pe.wait_ge(S["dv_qh"], g + 1)
                    pe.wait_ge(S["dv_minus"], g + 1)
                if not (isinstance(g, int) and NW * g + w < 2):
                    pe.wait_ge(S["ac_probs"], NW * g + w - 1)
                bank = psum[:, PROB0 + w % 2, :]
                pe.matmul(bank, k_blocks[:, par, w, :], q_heads[:, par, w, :, :], start=True, stop=False)
                pe.matmul(bank, reverse[:], rel[:, 1, :], start=False, stop=False)
                pe.matmul(bank, pick[:, w, :], minus_max[:, :, :], start=False, stop=True).then_inc(S["pe_scores"], 1)

            def weighted_values(g, quad, par):
                pe.wait_ge(S["ac_probs"], NW * g + 4 * quad + 4)
                if not (isinstance(g, int) and g == 0 and quad == 0):
                    pe.wait_ge(S["dv_att"], 2 * g + quad)
                for j in range(4):
                    for hh in range(2):
                        for p in range(4):
                            w, head = 4 * quad + p, 4 * hh + j
                            at = (w * NH + head) * 32 - 16 * hh
                            pe.matmul(psum[32 * p:32 * p + 32, PV, j * T:(j + 1) * T], v_blocks[:, par, at:at + 32],
                                      probs[:, w, head * T:(head + 1) * T], start=hh == 0, stop=hh == 1)
                for hh in range(2):
                    for p in range(4):
                        w = 4 * quad + p
                        a = _AT["ones_by_head_half"][0] + 32 * hh
                        ins = pe.matmul(psum[32 * p:32 * p + 32, PV, 256:512], consts[:, a:a + 32],
                                        probs[:, w, hh * 256:(hh + 1) * 256], start=hh == 0, stop=hh == 1)
                ins.then_inc(S["pe_pv"], 1)

            def projection(c):
                pe.wait_ge(S["dv_att"], 2 * (c + 1))
                if not (isinstance(c, int) and c == 0):
                    pe.wait_ge(S["ac_log2"], c)
                pe.matmul(psum[:, MISC1, :], proj_w[:], attended[:], start=True, stop=True).then_inc(S["pe_proj"], 1)

            def centered2(c):
                pe.wait_ge(S["dv_x1"], c + 1)
                if not (isinstance(c, int) and c == 0):
                    pe.wait_ge(S["dv_normed2"], c)
                pe.matmul(psum[:, NORM, :], const("center"), x1[:, bass.ds(c * G, G)], start=True, stop=True).then_inc(S["pe_xc2"], 1)

            def variance2(c):
                pe.wait_ge(S["ac_sq2"], c + 1)
                if not (isinstance(c, int) and c >= NG - 2):
                    pe.wait_ge(S["ac_k"], c + 3)
                else:
                    pe.wait_ge(S["ac_proj"], c + 1)
                pe.matmul(psum[:, MISC1, :], const("average"), square2, start=True, stop=True).then_inc(S["pe_var2"], 1)

            def step(g, nxt, prev, par):
                if nxt is not None:
                    centered(nxt)
                scores(g, 0, par)
                scores(g, 1, par)
                if nxt is not None:
                    variance(nxt)
                scores(g, 2, par)
                if prev is not None:
                    projection(prev)
                scores(g, 3, par)
                if nxt is not None:
                    qkv(nxt, second=isinstance(nxt, int) and nxt == 1)
                scores(g, 4, par)
                weighted_values(g, 0, par)
                if prev is not None:
                    centered2(prev)
                scores(g, 5, par)
                if prev is not None:
                    variance2(prev)
                if nxt is not None:
                    for w in range(2):
                        scores_for_max(nxt, w)
                scores(g, 6, par)
                if nxt is not None:
                    for w in range(2, 4):
                        scores_for_max(nxt, w)
                scores(g, 7, par)
                if nxt is not None:
                    for w in range(4, 8):
                        scores_for_max(nxt, w)
                weighted_values(g, 1, par)
                if nxt is not None:
                    transpose_maxima(nxt)

            pe.wait_ge(S["consts_in"], 32)
            pe.wait_ge(S["x_first"], 32)
            centered(0)
            pe.wait_ge(S["weights_in"], 16 * len(loads))
            for m in range(3):
                pe.matmul(psum[:, PV, m:m + 1], qkv_raw[:, m, :], vec[:, 1:2], start=True, stop=True)
            for f in range(2):
                ins = pe.matmul(psum[:, PV, 3 + f:4 + f], mlp1_raw[:, 0, f * 128:(f + 1) * 128], vec[:, 3:4], start=True, stop=True)
            ins.then_inc(S["setup_pe"], 1)
            pe.wait_ge(S["setup_dve"], 2)
            pe.matmul(psum[:, PV, 5:6], proj_raw, qkv_bias[:, 2:3], start=True, stop=True).then_inc(S["setup_pe"], 1)
            variance(0, first=True)
            pe.wait_ge(S["ready"], 1)
            qkv(0, first=True)
            pe.wait_ge(S["ready"], 2)
            for w in range(NW):
                scores_for_max(0, w)
            transpose_maxima(0)
            pe.wait_ge(S["x_rest"], 32 * (NB4 - 1))
            step(0, 1, None, 0)
            with pe.Fori(0, NG // 2 - 1) as i:
                step(2 * i + 1, 2 * i + 2, 2 * i, 1)
                step(2 * i + 2, 2 * i + 3, 2 * i + 1, 0)
            step(NG - 1, None, NG - 2, 1)
            projection(NG - 1)
            centered2(NG - 1)
            variance2(NG - 1)

            def mlp1(n, par):
                for m in range(4):
                    bh, f = m // 2, m % 2
                    if not (isinstance(n, int) and n == 0):
                        pe.wait_ge(S["ac_gelu"], 4 * n + m - 3)
                    pe.matmul(psum[:, m, :], mlp1_w[:, bh, f * 128:(f + 1) * 128], normed2[:, bass.ds(n * G, G)],
                              start=True, stop=True).then_inc(S["pe_mlp1"], 1)

            def mlp2(n, par):
                if not (isinstance(n, int) and n < 2):
                    pe.wait_ge(S["ac_mlp"], n - 1)
                for f in range(2):
                    for bh in range(2):
                        if f == 0:
                            pe.wait_ge(S["ac_gelu"], 4 * n + 2 * bh + 2)
                        ins = pe.matmul(psum[bh * C:(bh + 1) * C, 4 + par, :], mlp2_w[:, f, :], hidden[:, par, 2 * bh + f, :],
                                        start=f == 0, stop=f == 1)
                ins.then_inc(S["pe_mlp2"], 1)

            def pointwise1(n, half):
                pe.wait_ge(S["dv_x2"], 2 * (n + 1))
                pe.matmul(psum[:, 6 + half, :], pw1_w[:], x2[:, bass.ds(n * G, G)], start=True, stop=True).then_inc(S["pe_pw1"], 1)

            pe.wait_ge(S["dv_normed2"], NG)
            mlp1(0, 0)
            mlp1(1, 1)
            mlp2(0, 0)
            with pe.Fori(0, NG // 2 - 1) as i:
                mlp1(2 * i + 2, 0)
                mlp2(2 * i + 1, 1)
                pointwise1(2 * i, 0)
                mlp1(2 * i + 3, 1)
                mlp2(2 * i + 2, 0)
                pointwise1(2 * i + 1, 1)
            mlp2(NG - 1, 1)
            pointwise1(NG - 2, 0)
            pointwise1(NG - 1, 1)

            pe.wait_ge(S["gate_dve"], 1)
            pe.matmul(psum[:, 0, 0:B], fc1_w[:], gap[:], start=True, stop=True).then_inc(S["gate_pe"], 1)
            pe.wait_ge(S["gate_dve"], 2)
            for b in range(B):
                ins = pe.matmul(psum[:, 1, 6 * b:6 * b + 6], gap2_rep[:, b, :], off_w[:], start=True, stop=True)
            ins.then_inc(S["gate_pe"], 1)
            pe.wait_ge(S["gate_dve"], 3)
            pe.matmul(psum[0:B, 2, 0:C], fc1_out, fc2_w[:], start=True, stop=True).then_inc(S["gate_pe"], 1)
            pe.wait_ge(S["gate_dve"], 7)
            pe.matmul(psum[:, 3, :], ones8[:], score_diag, start=True, stop=True)
            pe.matmul(psum[:, 4, 0:B], score_rep, consts[0:B, _AT["batch_of_row"][0]:_AT["batch_of_row"][1]],
                      start=True, stop=True).then_inc(S["gate_pe"], 1)

            pe.wait_ge(S["gate_dve"], 12)
            for b4 in range(NB4):
                par = b4 % 2
                pe.wait_ge(S[f"shift_in{par}"], 128 * (b4 // 2 + 1))
                pe.wait_ge(S["dv_convw"], 2 * (b4 + 1))
                for half in range(2):
                    n = 2 * b4 + half
                    if n >= 2:
                        pe.wait_ge(S["dv_result"], n - 1)
                    for t in range(NKT):
                        dy, x0 = t // 2, 4 * (t % 2)
                        for bh in range(2):
                            img = shifted[:, par, bh, :].rearrange("p (y x) -> p y x", x=PW)
                            ins = pe.matmul(psum[bh * C:(bh + 1) * C, n % 2, :], conv_w[:, par, bh, t, :],
                                            img[:, half * 16 + dy:half * 16 + dy + 16, x0:x0 + W],
                                            start=t == 0, stop=t == NKT - 1)
                    ins.then_inc(S["pe_conv"], 1)

        @block.vector
        def _(dve):
            link_count = [0]

            dve.memset(eps[:], EPS1)
            dve.wait_ge(S["weights_in"], 16 * len(loads))
            dve.tensor_scalar(qkv_w[:], qkv_raw, vec[:, 0:1], None, ALU.mult)
            dve.tensor_scalar(mlp1_w[:], mlp1_raw, vec[:, 2:3], None, ALU.mult)
            dve.wait_ge(S["setup_pe"], 1)
            dve.tensor_tensor(qkv_bias[:], psum[:, PV, 0:3], vec[:, 4:7], ALU.add).then_inc(S["setup_dve"], 1)
            dve.tensor_tensor(mlp1_bias[:], psum[:, PV, 3:5], vec[:, 11:13], ALU.add).then_inc(S["setup_dve"], 1)
            dve.wait_ge(S["setup_dve"], 1)
            dve.tensor_scalar(q_bias[:], qkv_bias[:, 0:1], SCALE, None, ALU.mult)
            dve.wait_ge(S["setup_pe"], 2)
            dve.tensor_tensor(proj_bias[:], psum[:, PV, 5:6], vec[:, 7:8], ALU.add).then_inc(S["ready"], 1)

            def patches(n):
                return rel_raw[:, n, :, :].rearrange("p h (a b) -> p h a b", a=WS)[:, :, :, 0:WS]

            def split_bias():
                dve.wait_ge(S["rel_in"], 16 * len(rel_loads))
                dve.wait_ge(S["consts_in"], 32)
                for n in range(2):
                    ins = dve.tensor_copy(rel[0:T, n, :].rearrange("p (h a b) -> p h a b", h=NH, a=WS), patches(n))
                ins.then_inc(S["setup_dve"], 1)
                dve.tensor_copy(reverse[:], const("reverse"))
                dve.tensor_tensor(pick[:], const("window_of_row").unsqueeze(2).to_broadcast([128, NW, 128]),
                                  const("same_half").unsqueeze(1).to_broadcast([128, NW, 128]), ALU.mult)
                dve.wait_ge(S["setup_dve"], 3)
                for n in range(2):
                    high = rel[0:T, n, :].bitcast(F32).rearrange("p (h a b) -> p h a b", h=NH, a=WS)
                    ins = dve.tensor_tensor(rel[T:128, n, :].rearrange("p (h a b) -> p h a b", h=NH, a=WS),
                                            patches(n), high, ALU.subtract)
                ins.then_inc(S["ready"], 1)

            def normalise(n):
                dve.wait_ge(S["ac_rstd"], n + 1)
                dve.tensor_tensor(normed[:], psum[:, NORM, :], rstd[:], ALU.mult).then_inc(S["dv_normed"], 1)

            def expand(n, par, heads, q_side):
                pass

            def q_block(n):
                dve.wait_ge(S["ac_q"], n + 1)
                for bh in range(2):
                    r = slice(bh * C, (bh + 1) * C)
                    ins = dve.tensor_copy(q_blocks[r, :, bh * T:(bh + 1) * T], q[r, :].rearrange("p (w t) -> p w t", t=T))
                ins.then_inc(S["dv_qb"], 1)

            def k_head(n):
                dve.wait_ge(S["ac_k"], n + 1)
                for h in range(NH):
                    a = _AT["head_of_channel"][0] + h
                    ins = dve.tensor_scalar(k_heads[:, :, h, :], k[:].rearrange("p (w t) -> p w t", t=T),
                                            consts[:, a:a + 1], None, ALU.mult)
                ins.then_inc(S["dv_kh"], 1)

            def k_block(n, par):
                for bh in range(2):
                    r = slice(bh * C, (bh + 1) * C)
                    ins = dve.tensor_copy(k_blocks[r, par, :, bh * T:(bh + 1) * T], k[r, :].rearrange("p (w t) -> p w t", t=T))
                ins.then_inc(S["dv_kb"], 1)

            def q_head(n, par):
                for h in range(NH):
                    a = _AT["head_of_channel"][0] + h
                    ins = dve.tensor_scalar(q_heads[:, par, :, h, :], q[:].rearrange("p (w t) -> p w t", t=T),
                                            consts[:, a:a + 1], None, ALU.mult)
                ins.then_inc(S["dv_qh"], 1)

            def take_maximum(n, w):
                dve.wait_ge(S["pe_max"], NW * n + w + 1)
                dve.tensor_reduce(maxima[:, w * NH:(w + 1) * NH], psum[:, MAX0 + w % 2, :].rearrange("p (h t) -> p h t", t=T),
                                  AX.X, ALU.max).then_inc(S["dv_max"], 1)

            def spread_maxima(n):
                dve.wait_ge(S["pe_maxt"], n + 1)
                dve.tensor_scalar(maxima_t[0:C, :], psum[0:C, MISC0, 0:T], -1.0, None, ALU.mult)
                dve.tensor_scalar(maxima_t[C:128, :], psum[0:C, MISC0, T:2 * T], -1.0, None, ALU.mult).then_inc(S["dv_maxt"], 1)
                dve.wait_ge(S["dv_maxt"], n + 1)
                dve.tensor_tensor(minus_max[:], maxima_t[:].unsqueeze(1).to_broadcast([128, NH, T]),
                                  const("head_of_row").unsqueeze(2).to_broadcast([128, NH, T]), ALU.mult).then_inc(S["dv_minus"], 1)

            def divide_by_sums(g, quad):
                dve.wait_ge(S["pe_pv"], 2 * g + quad + 1)
                dve.reciprocal(inv_sum[:], psum[:, PV, 256:512]).then_inc(S["dv_inv"], 1)
                dve.wait_ge(S["dv_inv"], 2 * g + quad + 1)
                for j in range(4):
                    for p in range(4):
                        w = 4 * quad + p
                        ins = dve.tensor_tensor(attended[32 * j:32 * j + 32, w * T:(w + 1) * T],
                                                psum[32 * p:32 * p + 32, PV, j * T:(j + 1) * T],
                                                inv_sum[32 * p:32 * p + 32, j * T:(j + 1) * T], ALU.mult)
                ins.then_inc(S["dv_att"], 1)

            def add_residual(c):
                dve.wait_ge(S["ac_proj"], c + 1)
                for s in range(2):
                    o = x1[:, bass.ds(c * G + s * 256, 256)].rearrange("p (w a b) -> p w a b", a=WS, b=WS)
                    ins = dve.tensor_tensor(o, stripe(projected, s), x_view(c, s), ALU.add)
                ins.then_inc(S["dv_x1"], 1)

            def normalise2(c):
                dve.wait_ge(S["ac_rstd2"], c + 1)
                dve.tensor_tensor(normed2[:, bass.ds(c * G, G)], psum[:, NORM, :], rstd2[:], ALU.mult).then_inc(S["dv_normed2"], 1)

            def step(g, nxt, prev, par):
                if prev is not None and nxt is None:
                    add_residual(prev)
                if nxt is not None:
                    normalise(nxt)
                    if prev is not None:
                        add_residual(prev)
                    q_block(nxt)
                    k_head(nxt)
                divide_by_sums(g, 0)
                if nxt is not None:
                    k_block(nxt, 1 - par)
                    q_head(nxt, 1 - par)
                if prev is not None:
                    normalise2(prev)
                if nxt is not None:
                    for w in range(NW):
                        take_maximum(nxt, w)
                    spread_maxima(nxt)
                divide_by_sums(g, 1)

            normalise(0)
            dve.wait_ge(S["zeroed"], 9)
            q_block(0)
            k_head(0)
            split_bias()
            k_block(0, 0)
            q_head(0, 0)
            for w in range(NW):
                take_maximum(0, w)
            spread_maxima(0)
            step(0, 1, None, 0)
            with dve.Fori(0, NG // 2 - 1) as i:
                step(2 * i + 1, 2 * i + 2, 2 * i, 1)
                step(2 * i + 2, 2 * i + 3, 2 * i + 1, 0)
            step(NG - 1, None, NG - 2, 1)
            add_residual(NG - 1)
            normalise2(NG - 1)

            def add_mlp(n, par):
                dve.wait_ge(S["ac_mlp"], n + 1)
                for s in range(2):
                    o = x2[:, bass.ds(n * G + s * 256, 256)].rearrange("p (a w b) -> p w a b", a=WS, b=WS)
                    i1 = x1[:, bass.ds(n * G + s * 256, 256)].rearrange("p (w a b) -> p w a b", a=WS, b=WS)
                    dve.tensor_tensor(o, stripe(mlp_out[:, par, :], s), i1, ALU.add).then_inc(S["dv_x2"], 1)

            def pool_image(n, b4, half):
                dve.wait_ge(S["ac_relu"], n + 1)
                dve.tensor_reduce(h_sum[:, bass.ds(n, 1)], psum[:, 6 + half, :], AX.X, ALU.add).then_inc(S["dv_hsum"], 1)
                img = act_img[:, b4, 0:PIMG].rearrange("p (y x) -> p y x", x=PW)
                dve.tensor_reduce(r_sum[:, bass.ds(n, 1)], img[:, PAD + half * 16:PAD + half * 16 + 16, PAD:PAD + W],
                                  AX.XY, ALU.add).then_inc(S["dv_rsum"], 1)

            add_mlp(0, 0)
            with dve.Fori(0, NG // 2 - 1) as i:
                add_mlp(2 * i + 1, 1)
                pool_image(2 * i, i, 0)
                add_mlp(2 * i + 2, 0)
                pool_image(2 * i + 1, i, 1)
            add_mlp(NG - 1, 1)
            pool_image(NG - 2, NB4 - 1, 0)
            pool_image(NG - 1, NB4 - 1, 1)

            dve.wait_ge(S["zeroed"], NZERO)
            dve.wait_ge(S["dv_hsum"], NG)
            dve.wait_ge(S["dv_rsum"], NG)
            dve.tensor_reduce(pooled[:, 0, :], h_sum[:].rearrange("p (b s) -> p b s", s=2), AX.X, ALU.add)
            dve.tensor_reduce(pooled[:, 1, :], r_sum[:].rearrange("p (b s) -> p b s", s=2), AX.X, ALU.add).then_inc(S["dv_hsum"], 1)
            dve.wait_ge(S["dv_hsum"], NG + 1)
            for bh in range(2):
                r = slice(bh * C, (bh + 1) * C)
                dve.tensor_scalar(gap2[r, bh * NB4:(bh + 1) * NB4], pooled[r, 1, :], 1.0 / PIX, None, ALU.mult).then_inc(S["dv_rsum"], 1)
            for bh in range(2):
                r = slice(bh * C, (bh + 1) * C)
                ins = dve.tensor_scalar(gap[r, bh * NB4:(bh + 1) * NB4], pooled[r, 0, :], 1.0 / PIX, vec[r, 9:10], ALU.mult, ALU.add)
            ins.then_inc(S["gate_dve"], 1)
            dve.wait_ge(S["dv_rsum"], NG + 2)
            dve.tensor_copy(gap2_rep, gap2[:].unsqueeze(2).to_broadcast([128, B, 128])).then_inc(S["gate_dve"], 1)
            dve.wait_ge(S["gate_pe"], 1)
            dve.tensor_scalar(fc1_out, psum[:, 0, 0:B], vec[:, 13:14], 0.0, ALU.add, ALU.max).then_inc(S["gate_dve"], 1)
            dve.wait_ge(S["gate_pe"], 3)
            dve.tensor_tensor(score_row, psum[0:B, 2, 0:C], fc2_bias[:], ALU.add).then_inc(S["gate_dve"], 1)
            dve.tensor_tensor(offset, psum[:, 1, 0:6 * B].rearrange("p (b t) -> p b t", t=6),
                              off_bias[:].unsqueeze(1).to_broadcast([128, B, 6]), ALU.add).then_inc(S["gate_dve"], 1)
            dve.wait_ge(S["gate_act"], 1)
            dve.tensor_copy(score_rep, score_row[:, 0:KS].unsqueeze(1).to_broadcast([B, 4, KS])).then_inc(S["gate_dve"], 1)
            bor = consts[0:B, _AT["batch_of_row"][0]:_AT["batch_of_row"][1]]
            dve.tensor_tensor(score_diag, score_row.unsqueeze(1).to_broadcast([B, B, C]),
                              bor.unsqueeze(2).to_broadcast([B, B, C]), ALU.mult).then_inc(S["gate_dve"], 1)
            dve.wait_ge(S["gate_pe"], 4)
            dve.tensor_copy(score_col, psum[:, 4, 0:B]).then_inc(S["gate_dve"], 1)
            dve.wait_ge(S["gate_dve"], 8)
            col = score_col.unsqueeze(2).to_broadcast([128, B, C])
            every = psum[:, 3, :].rearrange("p (b c) -> p b c", c=C)
            dve.tensor_tensor(equal, every, col, ALU.is_equal).then_inc(S["gate_dve"], 1)
            dve.tensor_tensor(greater, every, col, ALU.is_gt)
            dve.wait_ge(S["gate_dve"], 9)
            dve.tensor_tensor(equal, equal, const("earlier").unsqueeze(1).to_broadcast([128, B, C]), ALU.mult).then_inc(S["gate_dve"], 1)
            dve.wait_ge(S["gate_dve"], 10)
            dve.tensor_tensor(greater, greater, equal, ALU.add).then_inc(S["gate_dve"], 1)
            dve.wait_ge(S["gate_dve"], 11)
            dve.tensor_reduce(rank, greater, AX.X, ALU.add).then_inc(S["gate_dve"], 1)
            dve.wait_ge(S["gate_dve"], 12)
            dve.tensor_scalar(rank, rank, float(KS), None, ALU.is_lt).then_inc(S["gate_dve"], 1)
            dve.wait_ge(S["gate_act"], 4)
            dve.tensor_scalar(gain, gain, 1.0, None, ALU.add).then_inc(S["gate_dve"], 1)
            dve.wait_ge(S["gate_dve"], 14)
            n = 14
            full = [128, B, NKT]
            for m in range(len(KERNELS)):
                a = _AT["valid"][0] + m * NKT
                t = tap_w[:, m, :, :]
                for o, i0, i1, op in ((t, taps[:, m, :].unsqueeze(1).to_broadcast(full), gain[:, :, 2 * m:2 * m + 1].to_broadcast(full), ALU.mult),
                                      (t, t, shift[:, :, 2 * m + 1:2 * m + 2].to_broadcast(full), ALU.add),
                                      (live, consts[:, a:a + NKT].unsqueeze(1).to_broadcast(full), rank.unsqueeze(2).to_broadcast(full), ALU.mult),
                                      (t, t, live, ALU.mult)):
                    dve.tensor_tensor(o, i0, i1, op).then_inc(S["gate_dve"], 1)
                    n += 1
                    dve.wait_ge(S["gate_dve"], n)

            def conv_weights(b4, bh, par, count):
                b = bh * NB4 + b4
                w = conv_w[:, par, bh, :, :]
                for m in (2, 1, 0):
                    o = (TAP - KERNELS[m]) // 2
                    lo, hi = 2 * o, 2 * (TAP - o)
                    shape = [128, hi - lo, C]
                    dst = (w if m == 2 else conv_t)[:, lo:hi, :]
                    dve.tensor_tensor(dst, tap_w[:, m, b, lo:hi].unsqueeze(2).to_broadcast(shape),
                                      fuse_w[:, m, :].unsqueeze(1).to_broadcast(shape), ALU.mult).then_inc(S["dv_mulw"], 1)
                    count += 1
                    dve.wait_ge(S["dv_mulw"], count)
                    if m != 2:
                        dve.tensor_tensor(w[:, lo:hi, :], w[:, lo:hi, :], conv_t[:, lo:hi, :], ALU.add).then_inc(S["dv_mulw"], 1)
                        count += 1
                        dve.wait_ge(S["dv_mulw"], count)
                return count

            count = 0
            for b4 in range(2):
                for bh in range(2):
                    count = conv_weights(b4, bh, b4, count)
                    dve.engine_nop().then_inc(S["dv_convw"], 1)
            for b4 in range(NB4):
                for half in range(2):
                    m = 2 * b4 + half
                    dve.wait_ge(S["pe_conv"], m + 1)
                    if m >= 2:
                        dve.wait_ge(S[f"out_done{half}"], 32 * b4)
                    dve.scalar_tensor_tensor(result[:, m % 2, :], psum[:, m % 2, :], vec[:, 10:11], x2[:, m * G:(m + 1) * G],
                                             ALU.add, ALU.add).then_inc(S["dv_result"], 1)
                if b4 + 2 < NB4:
                    for bh in range(2):
                        count = conv_weights(b4 + 2, bh, b4 % 2, count)
                        dve.engine_nop().then_inc(S["dv_convw"], 1)


_DIRECT = ["x", "w_qkv", "w_proj", "w_mlp1", "w_mlp2", "rel_table"]


def _layout(inputs):
    a = {k: np.asarray(v) for k, v in inputs.items()}
    L0, L1 = "L0_conv_", "L1_conv_"
    table = a[L0 + "rel_bias_table"].T.reshape(NH, 2 * WS - 1, 2 * WS - 1)
    kernels = []
    for k in KERNELS:
        o = (TAP - k) // 2
        w = np.pad(a[f"{L1}dw{k}"][:KS, 0], ((0, 0), (o, o), (o, o + 1)))
        kernels.append(w.reshape(KS, TAP, 2, 4).transpose(3, 0, 1, 2).reshape(128, NKT))
    column = lambda v: v.reshape(-1, 1)
    return {
        "x": a["x"].reshape(B, C, PIX),
        "consts": _constants(),
        "w_qkv": a[L0 + "w_qkv"], "w_proj": a[L0 + "w_proj"], "w_mlp1": a[L0 + "w_mlp1"], "w_mlp2": a[L0 + "w_mlp2"],
        "ln1_scale": column(a[L0 + "ln1_scale"]), "ln1_bias": column(a[L0 + "ln1_bias"]),
        "ln2_scale": column(a[L0 + "ln2_scale"]), "ln2_bias": column(a[L0 + "ln2_bias"]),
        "b_qkv": a[L0 + "b_qkv"].reshape(3, C).T, "b_proj": column(a[L0 + "b_proj"]),
        "b_mlp1": a[L0 + "b_mlp1"].reshape(2, 128).T, "b_mlp2": column(a[L0 + "b_mlp2"]),
        "rel_table": table, "rel_flipped": table[:, ::-1, ::-1],
        "pw1_t": a[L1 + "pw1_w"].T, "pw1_b": column(a[L1 + "pw1_b"]),
        "fc1_t": a[L1 + "fc1_w"].T, "fc1_b": column(a[L1 + "fc1_b"]),
        "fc2_t": a[L1 + "fc2_w"].T, "fc2_b": a[L1 + "fc2_b"],
        "off_t": a[L1 + "off_w"].T, "off_b": a[L1 + "off_b"],
        "fuse_t": a[L1 + "pw_w"][:, :3 * KS].T, "pw_b": column(a[L1 + "pw_b"]),
        "taps": np.stack(kernels, axis=1),
    }


def kernel(**inputs):
    import concourse.bacc as _bacc
    from concourse.bass_utils import run_bass_kernel_spmd as _run

    nc = _bacc.Bacc("TRN2", target_bir_lowering=False, num_devices=1)
    arrays, args = {}, {}
    for name, v in _layout(inputs).items():
        v = np.ascontiguousarray(v)
        arrays[f"in_{name}"] = v
        args[name] = nc.dram_tensor(f"in_{name}", v.shape, mybir.dt.from_np(v.dtype), kind="ExternalInput").ap()
    out = nc.dram_tensor("out", (B, C, PIX), mybir.dt.float32, kind="ExternalOutput").ap()
    conv_seq_kernel(nc, args, out)
    r = _run(nc, [arrays], core_ids=[0])
    return r.results[0]["out"].reshape(B, C, H, W)
```

```python
import numpy as np
import concourse.bass as bass
from concourse import mybir
from contextlib import ExitStack

B, C, H, W = 8, 64, 32, 32
WS, NH, HD = 8, 8, 8
NB4 = B // 2
PIX = H * W
COLS = NB4 * PIX
G = 512
NG = COLS // G
NW = G // (WS * WS)
T = WS * WS
HIDDEN = 4 * C
KS = C // 2
KERNELS = (3, 5, 7)
TAP = 7
PAD = TAP // 2
PATCH = WS * (2 * WS - 1)
PW = W + 2 * PAD
PIMG = PW * (H + 2 * PAD)
PBUF = PIMG + 4
NKT = 2 * TAP
EPS1 = 1e-5
SCALE = float(HD) ** -0.5

_p = np.arange(128)
_bh, _c = _p // C, _p % C


def _valid():
    v = np.zeros((128, len(KERNELS), TAP, 2), np.float32)
    for i, k in enumerate(KERNELS):
        o = (TAP - k) // 2
        for p in range(128):
            for half in range(2):
                dx = 4 * half + p // KS
                if o <= dx < TAP - o:
                    v[p, i, o:TAP - o, half] = 1
    return v.reshape(128, -1)


_CONST = {
    "center": np.where(_bh[:, None] == _bh, (_p[:, None] == _p) - 1.0 / C, 0),
    "average": np.where(_bh[:, None] == _bh, 1.0 / C, 0),
    "ident": _p[:, None] == _p,
    "reverse": (_p % T)[:, None] == T - 1 - _p % T,
    "head_of_channel": (_c // HD)[:, None] == np.arange(NH),
    "head_of_row": (_p % NH)[:, None] == np.arange(NH),
    "window_of_row": (_p // NH % NW)[:, None] == np.arange(NW),
    "same_half": _bh[:, None] == _bh,
    "ones_by_head_half": (np.arange(64) // 32 == np.arange(64) % 32 // 16)[None]
    & (_bh[:, None] == np.arange(64) % 16 // HD),
    "earlier": np.arange(C) < (_p % KS)[:, None],
    "valid": _valid(),
    "batch_of_row": _p[:, None] == np.arange(B),
}
_AT, _n = {}, 0
for _k, _v in _CONST.items():
    _AT[_k] = (_n, _n + _v.shape[1])
    _n += _v.shape[1]
NCONST = _n
NFIRST = _AT["average"][1]


_WEIGHTS = {"vec": 16, "proj_w": 128, "mlp2_w": 2 * C, "pw1_w": 128, "fc1_w": 2 * C, "fc2_w": C, "off_w": 6,
            "off_bias": 6, "fc2_bias": C, "fuse_w": 3 * C, "taps": 3 * NKT}
_RAW = {"qkv": 3 * 128, "proj": 128, "mlp1": 2 * HIDDEN}


def _columns(sizes):
    at, n = {}, 0
    for name, size in sizes.items():
        at[name] = (n, n + size)
        n += size
    return at, n


_WAT, NWEIGHT = _columns(_WEIGHTS)
_RAT, NRAW = _columns(_RAW)


def _constants():
    return np.ascontiguousarray(np.concatenate([np.asarray(v, np.float32) for v in _CONST.values()], axis=1))


def conv_seq_kernel(nc, d, out):
    F32, F32R = mybir.dt.float32, mybir.dt.float32r
    ALU, ACT, AX = mybir.AluOpType, mybir.ActivationFunctionType, mybir.AxisListType

    ctx = ExitStack()
    with ctx:
        def sb(name, shape, dt=F32):
            return ctx.enter_context(nc.sbuf_tensor(name, shape, dt))

        def sem(name):
            return ctx.enter_context(nc.semaphore(name))

        consts = sb("consts", [128, NCONST])

        def const(name):
            a, b = _AT[name]
            return consts[:, a:b]

        x = sb("x", [128, COLS])
        x1 = sb("x1", [128, COLS])
        x2 = x
        normed2 = sb("normed2", [128, COLS])
        weights = sb("weights", [128, NWEIGHT])

        def weight(name):
            a, b = _WAT[name]
            return weights[:, a:b]

        vec = weight("vec")
        proj_w = weight("proj_w")
        mlp2_w = weight("mlp2_w").rearrange("p (f c) -> p f c", f=2)
        pw1_w, fc1_w, fc2_w, off_w = (weight(n) for n in ("pw1_w", "fc1_w", "fc2_w", "off_w"))
        fuse_w = weight("fuse_w").rearrange("p (m c) -> p m c", c=C)
        taps = weight("taps").rearrange("p (m t) -> p m t", t=NKT)
        fc2_bias, off_bias = weight("fc2_bias")[0:B], weight("off_bias")
        qkv_w = sb("qkv_w", [128, 3, 128])
        mlp1_w = sb("mlp1_w", [128, 2, HIDDEN])
        qkv_bias = sb("qkv_bias", [128, 3])
        q_bias = sb("q_bias", [128, 1])
        proj_bias = sb("proj_bias", [128, 1])
        mlp1_bias = sb("mlp1_bias", [128, 2])
        eps = sb("eps", [128, 1])
        rel_raw = x1[0:T, 0:2 * NH * PATCH].rearrange("p (n f h) -> p n f h", n=2, h=NH)
        rel = sb("rel", [128, 2, NH * T], F32R)
        reverse = sb("reverse", [128, 128], F32R)
        pick = sb("pick", [128, NW, 128], F32R)
        square_logvar = sb("square_logvar", [128, 2, G])
        square, logvar = square_logvar[:, 0, :], square_logvar[:, 1, :]
        rstd = sb("rstd", [128, G])
        normed = sb("normed", [128, G])
        q = sb("q", [128, G])
        k = sb("k", [128, G])
        q_blocks = sb("q_blocks", [128, NW, 128], F32R)
        k_heads = sb("k_heads", [128, NW, NH, T], F32R)
        arena = sb("arena", [128, 18 * 1024])
        a0 = [0]

        def carve(*shape):
            n = int(np.prod(shape))
            a0[0] += n
            names = " ".join("abcdef"[:len(shape)])
            return arena[:, a0[0] - n:a0[0]].rearrange(f"p ({names}) -> p {names}", **dict(zip("abcdef", shape)))

        q_heads = carve(2, NW, NH, T)
        k_blocks = carve(2, NW, 128)
        probs = carve(NW, NH * T)
        v_blocks = carve(2, NW * NH * 32)
        a0[0] = 10 * 1024
        raw = carve(NRAW)
        qkv_raw, proj_raw, mlp1_raw = (raw[:, a:b] for a, b in _RAT.values())
        qkv_raw = qkv_raw.rearrange("p (i o) -> p i o", i=3)
        mlp1_raw = mlp1_raw.rearrange("p (b f) -> p b f", b=2)
        a0[0] = 0
        shifted = carve(2, 2, PIMG)
        conv_w = carve(2, 2, NKT, C)
        conv_t = carve(NKT, C)
        gap2_rep = carve(B, 128)
        greater, equal = carve(B, C), carve(B, C)
        score_diag = carve(B, C)[0:B]
        score_rep = carve(4, KS)[0:B]
        live = carve(B, NKT)
        tap_w = carve(3, B, NKT)
        score_row = carve(C)[0:B]
        offset = carve(B, 6)
        gain = carve(B, 6)
        shift = carve(B, 6)
        fc1_out = carve(B)
        score_col = carve(B)
        rank = carve(B)
        a0[0] = 14 * 1024
        hidden = carve(2, 4, G)
        maxima = sb("maxima", [128, NW * NH])
        maxima_t = sb("maxima_t", [128, T])
        minus_max = sb("minus_max", [128, NH, T], F32R)
        inv_sum = sb("inv_sum", [128, 4 * T])
        attended = sb("attended", [128, G])
        projected = sb("projected", [128, G])
        square_logvar2 = sb("square_logvar2", [128, 2, G])
        square2, logvar2 = square_logvar2[:, 0, :], square_logvar2[:, 1, :]
        mlp_out, result = square_logvar, square_logvar2
        rstd2 = sb("rstd2", [128, G])
        act_img = sb("act_img", [128, NB4, PBUF])
        h_sum = sb("h_sum", [128, NG])
        r_sum = sb("r_sum", [128, NG])
        pooled = sb("pooled", [128, 2, NB4])
        gap = sb("gap", [128, B])
        gap2 = sb("gap2", [128, B])
        ones8 = sb("ones8", [B, 128])

        psum = ctx.enter_context(nc.psum_tensor("psum", [128, 8, 512], F32))
        NORM, MISC0, MISC1, MAX0, PROB0, PV = 0, 1, 2, 3, 5, 7

        S = {n: sem(n) for n in (
            "zeroed", "eps_set", "center_in", "consts_in", "x_first", "x_rest", "qkv_in", "raw_in", "weights_in", "rel_in",
            "pe_qkv_bias", "dv_qkv_bias", "qkv_ready", "pe_biases", "weights_ready", "dv_rel_high", "rel_ready",
            "pe_xc", "pe_var", "pe_q", "pe_k", "pe_v", "pe_max", "pe_maxt", "pe_scores", "pe_pv", "pe_proj", "pe_xc2", "pe_var2",
            "ac_sq", "ac_log", "ac_rstd", "ac_q", "ac_k", "ac_v", "ac_probs", "ac_proj", "ac_sq2", "ac_log2", "ac_rstd2",
            "dv_normed", "dv_qb", "dv_kh", "dv_kb", "po_qh", "dv_max", "dv_maxt", "dv_minus", "dv_inv", "dv_att", "dv_x1", "dv_normed2",
            "pe_mlp1", "pe_mlp2", "pe_pw1", "ac_gelu", "ac_mlp", "ac_relu", "dv_x2", "dv_hsum", "dv_rsum",
            "gate_dve", "gate_pe", "gate_act", "dv_convw", "dv_mulw", "shift_in0", "shift_in1", "pe_conv", "dv_result", "out_done0", "out_done1")}

        def x_view(g, s):
            base = g * G + s * (G // 2)
            return x[:, bass.ds(base, G // 2)].rearrange("p (a w b) -> p w a b", a=WS, b=WS)

        def stripe(t, s):
            return t[:, s * (G // 2):(s + 1) * (G // 2)].rearrange("p (w a b) -> p w a b", a=WS, b=WS)

        block = ctx.enter_context(nc.Block())

        @block.sync
        def _(sp):
            def load_x(b4, columns, done):
                for bh in range(2):
                    sp.dma_start(x[bh * C:(bh + 1) * C, b4 * PIX + columns.start:b4 * PIX + columns.stop],
                                 d["x"][bh * NB4 + b4, :, columns]).then_inc(done, 16)

            load_x(0, slice(0, G), S["x_first"])
            sp.dma_start(consts[:, NFIRST:], d["consts"][:, NFIRST:]).then_inc(S["consts_in"], 16)
            side = 2 * WS - 1
            run = ((WS - 1) * side + WS) * NH
            for n, name in enumerate(("rel_flipped", "rel_table")):
                src = bass.AP(d[name].tensor, d[name].offset, [[side * NH, WS], [NH, WS], [1, run]])
                sp.dma_start(rel_raw[:, n, :, :].rearrange("p f h -> p (f h)")[:, 0:run], src).then_inc(S["rel_in"], 16)
            load_x(0, slice(G, PIX), S["x_rest"])
            for b4 in range(1, NB4):
                load_x(b4, slice(0, PIX), S["x_rest"])

            def copy_images(b4, par):
                for bh in range(2):
                    for r in range(4):
                        sp.dma_start(shifted[r * KS:(r + 1) * KS, par, bh, :],
                                     act_img[bh * C:bh * C + KS, b4, r:r + PIMG]).then_inc(S[f"shift_in{par}"], 16)

            sp.wait_ge(S["ac_relu"], NG)
            copy_images(0, 0)
            copy_images(1, 1)
            for b4 in range(NB4):
                for half in range(2):
                    n = 2 * b4 + half
                    sp.wait_ge(S["dv_result"], n + 1)
                    for bh in range(2):
                        sp.dma_start(out[bh * NB4 + b4, :, half * G:(half + 1) * G],
                                     result[bh * C:(bh + 1) * C, n % 2, :]).then_inc(S[f"out_done{half}"], 16)
                if b4 + 2 < NB4:
                    sp.wait_ge(S["pe_conv"], 2 * (b4 + 1))
                    copy_images(b4 + 2, b4 % 2)
            for half in range(2):
                sp.wait_ge(S[f"out_done{half}"], 32 * NB4)

        @block.gpsimd
        def _(pool):
            pool.memset(q_blocks[:].bitcast(F32), 0.0).then_inc(S["zeroed"], 1)
            for t in (v_blocks, k_blocks, gap[:], gap2[:], act_img[:]):
                pool.memset(t, 0.0).then_inc(S["zeroed"], 1)
            pool.memset(ones8[:], 1.0).then_inc(S["zeroed"], 1)

            def q_head(n, par):
                if not (isinstance(n, int) and n < 2):
                    pool.wait_ge(S["pe_scores"], NW * (n - 1))
                pool.wait_ge(S["ac_q"], n + 1)
                shape = [128, NW // 2, NH, T]
                for s in range(2):
                    r = slice(s * NW // 2, (s + 1) * NW // 2)
                    some = q[:].rearrange("p (w t) -> p w t", t=T)[:, r]
                    pool.tensor_tensor(q_heads[:, par, r], some.unsqueeze(2).to_broadcast(shape),
                                       const("head_of_channel").unsqueeze(1).unsqueeze(3).to_broadcast(shape),
                                       ALU.mult).then_inc(S["po_qh"], 1)

            pool.wait_ge(S["consts_in"], 16)
            q_head(0, 0)
            q_head(1, 1)
            with pool.Fori(0, NG // 2 - 1) as i:
                q_head(2 * i + 2, 0)
                q_head(2 * i + 3, 1)

        NBLOCKS, NZERO = 3, 7

        @block.scalar
        def _(act):
            act.dma_start(consts[:, 0:NFIRST], d["consts"][:, 0:NFIRST]).then_inc(S["center_in"], 16)
            act.dma_start(vec, d["weights"][:, 0:_WAT["vec"][1]]).then_inc(S["qkv_in"], 16)
            nqkv = _RAT["qkv"][1]
            act.dma_start(raw[:, 0:nqkv], d["raw"][:, 0:nqkv]).then_inc(S["qkv_in"], 16)
            act.dma_start(raw[:, nqkv:], d["raw"][:, nqkv:]).then_inc(S["raw_in"], 16)
            act.dma_start(weights[:, _WAT["vec"][1]:], d["weights"][:, _WAT["vec"][1]:]).then_inc(S["weights_in"], 16)

            def square_of_centered(n):
                act.wait_ge(S["pe_xc"], n + 1)
                act.activation(square, psum[:, NORM, :], ACT.Square).then_inc(S["ac_sq"], 1)

            def inverse_deviation(n):
                act.wait_ge(S["pe_var"], n + 1)
                act.activation(logvar, psum[:, MISC0, :], ACT.Ln, bias=eps[:, 0:1]).then_inc(S["ac_log"], 1)
                act.wait_ge(S["ac_log"], n + 1)
                act.activation(rstd[:], logvar, ACT.Exp, scale=-0.5).then_inc(S["ac_rstd"], 1)

            def evacuate_qkv(n, par):
                act.wait_ge(S["pe_q"], n + 1)
                if not (isinstance(n, int) and n == 0):
                    act.wait_ge(S["po_qh"], 2 * n)
                act.activation(q[:], psum[:, MISC0, :], ACT.Identity, bias=q_bias[:, 0:1], scale=SCALE).then_inc(S["ac_q"], 1)
                act.wait_ge(S["pe_k"], n + 1)
                act.activation(k[:], psum[:, MISC1, :], ACT.Identity, bias=qkv_bias[:, 1:2]).then_inc(S["ac_k"], 1)
                act.wait_ge(S["pe_v"], n + 1)
                vb = v_blocks[:, par, :].rearrange("p (w two h e) -> p w two h e", two=2, h=NH, e=32)
                vp = psum[:, MAX0 + 1, :].rearrange("p (w b h e) -> p w b h e", b=2, h=NH, e=HD)
                for odd in range(2):
                    for bh in range(2):
                        act.copy(vb[bh * C:(bh + 1) * C, :, odd, :, bh * HD:(bh + 1) * HD],
                                 vp[odd * T:(odd + 1) * T, :, bh, :, :]).then_inc(S["ac_v"], 1)

            def exponentials(g, w):
                act.wait_ge(S["pe_scores"], NW * g + w + 1)
                act.activation(probs[:, w, :], psum[:, PROB0 + w % 2, :], ACT.Exp).then_inc(S["ac_probs"], 1)

            def evacuate_projection(c):
                act.wait_ge(S["pe_proj"], c + 1)
                act.activation(projected[:], psum[:, MISC1, :], ACT.Identity, bias=proj_bias[:, 0:1]).then_inc(S["ac_proj"], 1)

            def square_of_centered2(c):
                act.wait_ge(S["pe_xc2"], c + 1)
                act.activation(square2, psum[:, NORM, :], ACT.Square).then_inc(S["ac_sq2"], 1)

            def inverse_deviation2(c):
                act.wait_ge(S["pe_var2"], c + 1)
                act.activation(logvar2, psum[:, MISC1, :], ACT.Ln, bias=eps[:, 0:1]).then_inc(S["ac_log2"], 1)
                act.wait_ge(S["ac_log2"], c + 1)
                act.activation(rstd2[:], logvar2, ACT.Exp, scale=-0.5).then_inc(S["ac_rstd2"], 1)

            def step(g, nxt, prev, par):
                if nxt is not None:
                    square_of_centered(nxt)
                exponentials(g, 0)
                exponentials(g, 1)
                if nxt is not None:
                    inverse_deviation(nxt)
                exponentials(g, 2)
                if prev is not None:
                    evacuate_projection(prev)
                exponentials(g, 3)
                if nxt is not None:
                    evacuate_qkv(nxt, 1 - par)
                exponentials(g, 4)
                if prev is not None:
                    square_of_centered2(prev)
                exponentials(g, 5)
                if prev is not None:
                    inverse_deviation2(prev)
                exponentials(g, 6)
                exponentials(g, 7)

            act.add_instruction(mybir.InstLoadActFuncSet(name=nc.get_next_instruction_name(), engine=mybir.EngineType.Activation, act_func_set_id=6))
            square_of_centered(0)
            act.wait_ge(S["eps_set"], 1)
            inverse_deviation(0)
            act.wait_ge(S["qkv_ready"], 1)
            act.wait_ge(S["zeroed"], NBLOCKS)
            evacuate_qkv(0, 0)
            act.wait_ge(S["weights_ready"], 1)
            step(0, 1, None, 0)
            with act.Fori(0, NG // 2 - 1) as i:
                step(2 * i + 1, 2 * i + 2, 2 * i, 1)
                step(2 * i + 2, 2 * i + 3, 2 * i + 1, 0)
            step(NG - 1, None, NG - 2, 1)
            evacuate_projection(NG - 1)
            square_of_centered2(NG - 1)
            inverse_deviation2(NG - 1)

            def gelu(n, par):
                for m in range(4):
                    act.wait_ge(S["pe_mlp1"], 4 * n + m + 1)
                    act.activation(hidden[:, par, m, :], psum[:, m, :], ACT.Gelu, bias=mlp1_bias[:, m % 2:m % 2 + 1]).then_inc(S["ac_gelu"], 1)

            def evacuate_mlp(n, par):
                act.wait_ge(S["pe_mlp2"], n + 1)
                act.activation(mlp_out[:, par, :], psum[:, 4 + par, :], ACT.Identity, bias=vec[:, 8:9]).then_inc(S["ac_mlp"], 1)

            def relu(n, b4, half):
                act.wait_ge(S["pe_pw1"], n + 1)
                img = act_img[:, b4, 0:PIMG].rearrange("p (y x) -> p y x", x=PW)
                act.activation(img[:, PAD + half * 16:PAD + half * 16 + 16, PAD:PAD + W],
                               psum[:, 6 + half, :].rearrange("p (y x) -> p y x", x=W), ACT.Relu, bias=vec[:, 9:10]).then_inc(S["ac_relu"], 1)

            act.wait_ge(S["zeroed"], NZERO)
            gelu(0, 0)
            gelu(1, 1)
            evacuate_mlp(0, 0)
            with act.Fori(0, NG // 2 - 1) as i:
                gelu(2 * i + 2, 0)
                evacuate_mlp(2 * i + 1, 1)
                relu(2 * i, i, 0)
                gelu(2 * i + 3, 1)
                evacuate_mlp(2 * i + 2, 0)
                relu(2 * i + 1, i, 1)
            evacuate_mlp(NG - 1, 1)
            relu(NG - 2, NB4 - 1, 0)
            relu(NG - 1, NB4 - 1, 1)

            act.wait_ge(S["gate_dve"], 4)
            act.activation(score_row, score_row, ACT.Sigmoid).then_inc(S["gate_act"], 1)
            act.wait_ge(S["gate_dve"], 5)
            act.activation(offset, offset, ACT.Tanh).then_inc(S["gate_act"], 1)
            act.wait_ge(S["gate_act"], 2)
            act.activation(gain, offset, ACT.Sigmoid).then_inc(S["gate_act"], 1)
            act.activation(shift, offset, ACT.Tanh).then_inc(S["gate_act"], 1)

        @block.tensor
        def _(pe):
            def centered(n):
                for s in range(2):
                    ins = pe.matmul(psum[:, NORM, s * 256:(s + 1) * 256], const("center"), x_view(n, s), start=True, stop=True)
                ins.then_inc(S["pe_xc"], 1)

            def variance(n, first=False):
                pe.wait_ge(S["ac_sq"], n + 1)
                if not first:
                    pe.wait_ge(S["dv_maxt"], n)
                pe.matmul(psum[:, MISC0, :], const("average"), square, start=True, stop=True).then_inc(S["pe_var"], 1)

            def qkv(n, first=False, second=False):
                pe.wait_ge(S["dv_normed"], n + 1)
                pe.matmul(psum[:, MISC0, :], qkv_w[:, 0, :], normed[:], start=True, stop=True).then_inc(S["pe_q"], 1)
                if not (first or second):
                    pe.wait_ge(S["ac_proj"], n - 1)
                pe.matmul(psum[:, MISC1, :], qkv_w[:, 1, :], normed[:], start=True, stop=True).then_inc(S["pe_k"], 1)
                if not first:
                    pe.wait_ge(S["dv_max"], NW * n)
                for m in range(4):
                    ins = pe.matmul(psum[:, MAX0 + 1, m * 128:(m + 1) * 128], normed[:, m * 128:(m + 1) * 128],
                                    qkv_w[:, 2, :], start=True, stop=True)
                ins.then_inc(S["pe_v"], 1)

            def scores_for_max(n, w):
                if w == 0:
                    pe.wait_ge(S["dv_qb"], n + 1)
                    pe.wait_ge(S["dv_kh"], n + 1)
                if w == 1:
                    pe.wait_ge(S["ac_v"], 4 * (n + 1))
                if w >= 2:
                    pe.wait_ge(S["dv_max"], NW * n + w - 1)
                pe.matmul(psum[:, MAX0 + w % 2, :], q_blocks[:, w, :], k_heads[:, w, :, :], start=True, stop=False)
                pe.matmul(psum[:, MAX0 + w % 2, :], reverse[:], rel[:, 0, :], start=False, stop=True).then_inc(S["pe_max"], 1)

            def transpose_maxima(n):
                pe.wait_ge(S["dv_max"], NW * (n + 1))
                pe.wait_ge(S["ac_q"], n + 1)
                pe.matmul(psum[0:C, MISC0, 0:128], maxima[:], const("ident"), start=True, stop=True).then_inc(S["pe_maxt"], 1)

            def scores(g, w, par):
                if w == 0:
                    pe.wait_ge(S["dv_kb"], g + 1)
                    pe.wait_ge(S["po_qh"], 2 * g + 1)
                    pe.wait_ge(S["dv_minus"], g + 1)
                if not (isinstance(g, int) and NW * g + w < 2):
                    pe.wait_ge(S["ac_probs"], NW * g + w - 1)
                if w == NW // 2:
                    pe.wait_ge(S["po_qh"], 2 * g + 2)
                bank = psum[:, PROB0 + w % 2, :]
                pe.matmul(bank, k_blocks[:, par, w, :], q_heads[:, par, w, :, :], start=True, stop=False)
                pe.matmul(bank, reverse[:], rel[:, 1, :], start=False, stop=False)
                pe.matmul(bank, pick[:, w, :], minus_max[:, :, :], start=False, stop=True).then_inc(S["pe_scores"], 1)

            def weighted_values(g, quad, par):
                pe.wait_ge(S["ac_probs"], NW * g + 4 * quad + 4)
                if not (isinstance(g, int) and g == 0 and quad == 0):
                    pe.wait_ge(S["dv_att"], 2 * g + quad)
                for j in range(4):
                    for hh in range(2):
                        for p in range(4):
                            w, head = 4 * quad + p, 4 * hh + j
                            at = (w * NH + head) * 32 - 16 * hh
                            pe.matmul(psum[32 * p:32 * p + 32, PV, j * T:(j + 1) * T], v_blocks[:, par, at:at + 32],
                                      probs[:, w, head * T:(head + 1) * T], start=hh == 0, stop=hh == 1)
                for hh in range(2):
                    for p in range(4):
                        w = 4 * quad + p
                        a = _AT["ones_by_head_half"][0] + 32 * hh
                        ins = pe.matmul(psum[32 * p:32 * p + 32, PV, 256:512], consts[:, a:a + 32],
                                        probs[:, w, hh * 256:(hh + 1) * 256], start=hh == 0, stop=hh == 1)
                ins.then_inc(S["pe_pv"], 1)

            def projection(c):
                pe.wait_ge(S["dv_att"], 2 * (c + 1))
                pe.matmul(psum[:, MISC1, :], proj_w, attended[:], start=True, stop=True).then_inc(S["pe_proj"], 1)

            def centered2(c):
                pe.wait_ge(S["dv_x1"], c + 1)
                pe.matmul(psum[:, NORM, :], const("center"), x1[:, bass.ds(c * G, G)], start=True, stop=True).then_inc(S["pe_xc2"], 1)

            def variance2(c):
                pe.wait_ge(S["ac_sq2"], c + 1)
                if not (isinstance(c, int) and c >= NG - 2):
                    pe.wait_ge(S["ac_k"], c + 3)
                else:
                    pe.wait_ge(S["ac_proj"], c + 1)
                pe.matmul(psum[:, MISC1, :], const("average"), square2, start=True, stop=True).then_inc(S["pe_var2"], 1)

            def step(g, nxt, prev, par):
                if nxt is not None:
                    centered(nxt)
                scores(g, 0, par)
                scores(g, 1, par)
                if nxt is not None:
                    variance(nxt)
                scores(g, 2, par)
                if prev is not None:
                    projection(prev)
                scores(g, 3, par)
                if nxt is not None:
                    qkv(nxt, second=isinstance(nxt, int) and nxt == 1)
                scores(g, 4, par)
                weighted_values(g, 0, par)
                if prev is not None:
                    centered2(prev)
                scores(g, 5, par)
                if prev is not None:
                    variance2(prev)
                if nxt is not None:
                    for w in range(2):
                        scores_for_max(nxt, w)
                scores(g, 6, par)
                if nxt is not None:
                    for w in range(2, 4):
                        scores_for_max(nxt, w)
                scores(g, 7, par)
                if nxt is not None:
                    for w in range(4, 8):
                        scores_for_max(nxt, w)
                weighted_values(g, 1, par)
                if nxt is not None:
                    transpose_maxima(nxt)

            pe.wait_ge(S["center_in"], 16)
            pe.wait_ge(S["x_first"], 32)
            centered(0)
            pe.wait_ge(S["qkv_in"], 32)
            for m in range(3):
                ins = pe.matmul(psum[:, PV, m:m + 1], qkv_raw[:, m, :], vec[:, 1:2], start=True, stop=True)
            ins.then_inc(S["pe_qkv_bias"], 1)
            variance(0, first=True)
            pe.wait_ge(S["qkv_ready"], 1)
            qkv(0, first=True)
            pe.wait_ge(S["raw_in"], 16)
            for f in range(2):
                pe.matmul(psum[:, PV, 3 + f:4 + f], mlp1_raw[:, 0, f * 128:(f + 1) * 128], vec[:, 3:4], start=True, stop=True)
            pe.matmul(psum[:, PV, 5:6], proj_raw, qkv_bias[:, 2:3], start=True, stop=True).then_inc(S["pe_biases"], 1)
            pe.wait_ge(S["rel_ready"], 1)
            for w in range(NW):
                scores_for_max(0, w)
            transpose_maxima(0)
            pe.wait_ge(S["weights_in"], 16)
            pe.wait_ge(S["weights_ready"], 1)
            pe.wait_ge(S["x_rest"], 32 * NB4)
            step(0, 1, None, 0)
            with pe.Fori(0, NG // 2 - 1) as i:
                step(2 * i + 1, 2 * i + 2, 2 * i, 1)
                step(2 * i + 2, 2 * i + 3, 2 * i + 1, 0)
            step(NG - 1, None, NG - 2, 1)
            projection(NG - 1)
            centered2(NG - 1)
            variance2(NG - 1)

            def mlp1(n, par):
                for m in range(4):
                    bh, f = m // 2, m % 2
                    if not (isinstance(n, int) and n == 0):
                        pe.wait_ge(S["ac_gelu"], 4 * n + m - 3)
                    pe.matmul(psum[:, m, :], mlp1_w[:, bh, f * 128:(f + 1) * 128], normed2[:, bass.ds(n * G, G)],
                              start=True, stop=True).then_inc(S["pe_mlp1"], 1)

            def mlp2(n, par):
                for f in range(2):
                    for bh in range(2):
                        if f == 0:
                            pe.wait_ge(S["ac_gelu"], 4 * n + 2 * bh + 2)
                        ins = pe.matmul(psum[bh * C:(bh + 1) * C, 4 + par, :], mlp2_w[:, f, :], hidden[:, par, 2 * bh + f, :],
                                        start=f == 0, stop=f == 1)
                ins.then_inc(S["pe_mlp2"], 1)

            def pointwise1(n, half):
                pe.wait_ge(S["dv_x2"], 2 * (n + 1))
                pe.matmul(psum[:, 6 + half, :], pw1_w, x2[:, bass.ds(n * G, G)], start=True, stop=True).then_inc(S["pe_pw1"], 1)

            pe.wait_ge(S["dv_normed2"], NG)
            mlp1(0, 0)
            mlp1(1, 1)
            mlp2(0, 0)
            with pe.Fori(0, NG // 2 - 1) as i:
                mlp1(2 * i + 2, 0)
                mlp2(2 * i + 1, 1)
                pointwise1(2 * i, 0)
                mlp1(2 * i + 3, 1)
                mlp2(2 * i + 2, 0)
                pointwise1(2 * i + 1, 1)
            mlp2(NG - 1, 1)
            pointwise1(NG - 2, 0)
            pointwise1(NG - 1, 1)

            pe.wait_ge(S["gate_dve"], 1)
            pe.matmul(psum[:, 0, 0:B], fc1_w, gap[:], start=True, stop=True).then_inc(S["gate_pe"], 1)
            pe.wait_ge(S["gate_dve"], 2)
            for b in range(B):
                ins = pe.matmul(psum[:, 1, 6 * b:6 * b + 6], gap2_rep[:, b, :], off_w, start=True, stop=True)
            ins.then_inc(S["gate_pe"], 1)
            pe.wait_ge(S["gate_dve"], 3)
            pe.matmul(psum[0:B, 2, 0:C], fc1_out, fc2_w, start=True, stop=True).then_inc(S["gate_pe"], 1)
            pe.wait_ge(S["gate_dve"], 7)
            pe.matmul(psum[:, 3, :], ones8[:], score_diag, start=True, stop=True)
            pe.matmul(psum[:, 4, 0:B], score_rep, consts[0:B, _AT["batch_of_row"][0]:_AT["batch_of_row"][1]],
                      start=True, stop=True).then_inc(S["gate_pe"], 1)

            pe.wait_ge(S["gate_dve"], 12)
            for b4 in range(NB4):
                par = b4 % 2
                pe.wait_ge(S[f"shift_in{par}"], 128 * (b4 // 2 + 1))
                pe.wait_ge(S["dv_convw"], 2 * (b4 + 1))
                for half in range(2):
                    n = 2 * b4 + half
                    if n >= 2:
                        pe.wait_ge(S["dv_result"], n - 1)
                    for t in range(NKT):
                        dy, x0 = t // 2, 4 * (t % 2)
                        for bh in range(2):
                            img = shifted[:, par, bh, :].rearrange("p (y x) -> p y x", x=PW)
                            ins = pe.matmul(psum[bh * C:(bh + 1) * C, n % 2, :], conv_w[:, par, bh, t, :],
                                            img[:, half * 16 + dy:half * 16 + dy + 16, x0:x0 + W],
                                            start=t == 0, stop=t == NKT - 1)
                    ins.then_inc(S["pe_conv"], 1)

        @block.vector
        def _(dve):
            dve.memset(eps[:], EPS1).then_inc(S["eps_set"], 1)
            dve.wait_ge(S["qkv_in"], 32)
            dve.tensor_scalar(qkv_w[:], qkv_raw, vec[:, 0:1], None, ALU.mult)
            dve.wait_ge(S["pe_qkv_bias"], 1)
            dve.tensor_tensor(qkv_bias[:], psum[:, PV, 0:3], vec[:, 4:7], ALU.add).then_inc(S["dv_qkv_bias"], 1)
            dve.wait_ge(S["dv_qkv_bias"], 1)
            dve.tensor_scalar(q_bias[:], qkv_bias[:, 0:1], SCALE, None, ALU.mult).then_inc(S["qkv_ready"], 1)

            def other_weights():
                dve.wait_ge(S["raw_in"], 16)
                dve.tensor_scalar(mlp1_w[:], mlp1_raw, vec[:, 2:3], None, ALU.mult)
                dve.wait_ge(S["pe_biases"], 1)
                dve.tensor_tensor(mlp1_bias[:], psum[:, PV, 3:5], vec[:, 11:13], ALU.add)
                dve.tensor_tensor(proj_bias[:], psum[:, PV, 5:6], vec[:, 7:8], ALU.add).then_inc(S["weights_ready"], 1)

            def patches(n):
                return rel_raw[:, n, :, :].rearrange("p (a b) h -> p h a b", a=WS)[:, :, :, 0:WS]

            def split_bias():
                dve.wait_ge(S["rel_in"], 32)
                dve.wait_ge(S["consts_in"], 16)
                for n in range(2):
                    ins = dve.tensor_copy(rel[0:T, n, :].rearrange("p (h a b) -> p h a b", h=NH, a=WS), patches(n))
                ins.then_inc(S["dv_rel_high"], 1)
                dve.tensor_copy(reverse[:], const("reverse"))
                dve.tensor_tensor(pick[:], const("window_of_row").unsqueeze(2).to_broadcast([128, NW, 128]),
                                  const("same_half").unsqueeze(1).to_broadcast([128, NW, 128]), ALU.mult)
                dve.wait_ge(S["dv_rel_high"], 1)
                for n in range(2):
                    high = rel[0:T, n, :].bitcast(F32).rearrange("p (h a b) -> p h a b", h=NH, a=WS)
                    ins = dve.tensor_tensor(rel[T:128, n, :].rearrange("p (h a b) -> p h a b", h=NH, a=WS),
                                            patches(n), high, ALU.subtract)
                ins.then_inc(S["rel_ready"], 1)

            def normalise(n):
                dve.wait_ge(S["ac_rstd"], n + 1)
                dve.tensor_tensor(normed[:], psum[:, NORM, :], rstd[:], ALU.mult).then_inc(S["dv_normed"], 1)

            def q_block(n):
                dve.wait_ge(S["ac_q"], n + 1)
                for bh in range(2):
                    r = slice(bh * C, (bh + 1) * C)
                    ins = dve.tensor_copy(q_blocks[r, :, bh * T:(bh + 1) * T], q[r, :].rearrange("p (w t) -> p w t", t=T))
                ins.then_inc(S["dv_qb"], 1)

            def k_head(n):
                dve.wait_ge(S["ac_k"], n + 1)
                for h in range(NH):
                    a = _AT["head_of_channel"][0] + h
                    ins = dve.tensor_scalar(k_heads[:, :, h, :], k[:].rearrange("p (w t) -> p w t", t=T),
                                            consts[:, a:a + 1], None, ALU.mult)
                ins.then_inc(S["dv_kh"], 1)

            def k_block(n, par):
                for bh in range(2):
                    r = slice(bh * C, (bh + 1) * C)
                    ins = dve.tensor_copy(k_blocks[r, par, :, bh * T:(bh + 1) * T], k[r, :].rearrange("p (w t) -> p w t", t=T))
                ins.then_inc(S["dv_kb"], 1)

            def take_maximum(n, w):
                dve.wait_ge(S["pe_max"], NW * n + w + 1)
                dve.tensor_reduce(maxima[:, w * NH:(w + 1) * NH], psum[:, MAX0 + w % 2, :].rearrange("p (h t) -> p h t", t=T),
                                  AX.X, ALU.max).then_inc(S["dv_max"], 1)

            def spread_maxima(n):
                dve.wait_ge(S["pe_maxt"], n + 1)
                dve.tensor_scalar(maxima_t[0:C, :], psum[0:C, MISC0, 0:T], -1.0, None, ALU.mult)
                dve.tensor_scalar(maxima_t[C:128, :], psum[0:C, MISC0, T:2 * T], -1.0, None, ALU.mult).then_inc(S["dv_maxt"], 1)
                dve.wait_ge(S["dv_maxt"], n + 1)
                dve.tensor_tensor(minus_max[:], maxima_t[:].unsqueeze(1).to_broadcast([128, NH, T]),
                                  const("head_of_row").unsqueeze(2).to_broadcast([128, NH, T]), ALU.mult).then_inc(S["dv_minus"], 1)

            def divide_by_sums(g, quad):
                dve.wait_ge(S["pe_pv"], 2 * g + quad + 1)
                dve.reciprocal(inv_sum[:], psum[:, PV, 256:512]).then_inc(S["dv_inv"], 1)
                dve.wait_ge(S["dv_inv"], 2 * g + quad + 1)
                for j in range(4):
                    for p in range(4):
                        w = 4 * quad + p
                        ins = dve.tensor_tensor(attended[32 * j:32 * j + 32, w * T:(w + 1) * T],
                                                psum[32 * p:32 * p + 32, PV, j * T:(j + 1) * T],
                                                inv_sum[32 * p:32 * p + 32, j * T:(j + 1) * T], ALU.mult)
                ins.then_inc(S["dv_att"], 1)

            def add_residual(c):
                dve.wait_ge(S["ac_proj"], c + 1)
                for s in range(2):
                    o = x1[:, bass.ds(c * G + s * 256, 256)].rearrange("p (w a b) -> p w a b", a=WS, b=WS)
                    ins = dve.tensor_tensor(o, stripe(projected, s), x_view(c, s), ALU.add)
                ins.then_inc(S["dv_x1"], 1)

            def normalise2(c):
                dve.wait_ge(S["ac_rstd2"], c + 1)
                dve.tensor_tensor(normed2[:, bass.ds(c * G, G)], psum[:, NORM, :], rstd2[:], ALU.mult).then_inc(S["dv_normed2"], 1)

            def step(g, nxt, prev, par):
                if nxt is not None:
                    normalise(nxt)
                if prev is not None:
                    add_residual(prev)
                if nxt is not None:
                    q_block(nxt)
                    k_head(nxt)
                    k_block(nxt, 1 - par)
                divide_by_sums(g, 0)
                if nxt is not None:
                    take_maximum(nxt, 0)
                    take_maximum(nxt, 1)
                if prev is not None:
                    normalise2(prev)
                if nxt is not None:
                    for w in range(2, NW):
                        take_maximum(nxt, w)
                    spread_maxima(nxt)
                divide_by_sums(g, 1)

            split_bias()
            normalise(0)
            dve.wait_ge(S["zeroed"], NBLOCKS)
            q_block(0)
            k_head(0)
            other_weights()
            k_block(0, 0)
            for w in range(NW):
                take_maximum(0, w)
            spread_maxima(0)
            step(0, 1, None, 0)
            with dve.Fori(0, NG // 2 - 1) as i:
                step(2 * i + 1, 2 * i + 2, 2 * i, 1)
                step(2 * i + 2, 2 * i + 3, 2 * i + 1, 0)
            step(NG - 1, None, NG - 2, 1)
            add_residual(NG - 1)
            normalise2(NG - 1)

            def add_mlp(n, par):
                dve.wait_ge(S["ac_mlp"], n + 1)
                for s in range(2):
                    o = x2[:, bass.ds(n * G + s * 256, 256)].rearrange("p (a w b) -> p w a b", a=WS, b=WS)
                    i1 = x1[:, bass.ds(n * G + s * 256, 256)].rearrange("p (w a b) -> p w a b", a=WS, b=WS)
                    dve.tensor_tensor(o, stripe(mlp_out[:, par, :], s), i1, ALU.add).then_inc(S["dv_x2"], 1)

            def pool_image(n, b4, half):
                dve.wait_ge(S["ac_relu"], n + 1)
                dve.tensor_reduce(h_sum[:, bass.ds(n, 1)], psum[:, 6 + half, :], AX.X, ALU.add).then_inc(S["dv_hsum"], 1)
                img = act_img[:, b4, 0:PIMG].rearrange("p (y x) -> p y x", x=PW)
                dve.tensor_reduce(r_sum[:, bass.ds(n, 1)], img[:, PAD + half * 16:PAD + half * 16 + 16, PAD:PAD + W],
                                  AX.XY, ALU.add).then_inc(S["dv_rsum"], 1)

            add_mlp(0, 0)
            with dve.Fori(0, NG // 2 - 1) as i:
                add_mlp(2 * i + 1, 1)
                pool_image(2 * i, i, 0)
                add_mlp(2 * i + 2, 0)
                pool_image(2 * i + 1, i, 1)
            add_mlp(NG - 1, 1)
            pool_image(NG - 2, NB4 - 1, 0)
            pool_image(NG - 1, NB4 - 1, 1)

            dve.wait_ge(S["zeroed"], NZERO)
            dve.wait_ge(S["dv_hsum"], NG)
            dve.wait_ge(S["dv_rsum"], NG)
            dve.tensor_reduce(pooled[:, 0, :], h_sum[:].rearrange("p (b s) -> p b s", s=2), AX.X, ALU.add)
            dve.tensor_reduce(pooled[:, 1, :], r_sum[:].rearrange("p (b s) -> p b s", s=2), AX.X, ALU.add).then_inc(S["dv_hsum"], 1)
            dve.wait_ge(S["dv_hsum"], NG + 1)
            for bh in range(2):
                r = slice(bh * C, (bh + 1) * C)
                dve.tensor_scalar(gap2[r, bh * NB4:(bh + 1) * NB4], pooled[r, 1, :], 1.0 / PIX, None, ALU.mult).then_inc(S["dv_rsum"], 1)
            for bh in range(2):
                r = slice(bh * C, (bh + 1) * C)
                ins = dve.tensor_scalar(gap[r, bh * NB4:(bh + 1) * NB4], pooled[r, 0, :], 1.0 / PIX, vec[r, 9:10], ALU.mult, ALU.add)
            ins.then_inc(S["gate_dve"], 1)
            dve.wait_ge(S["dv_rsum"], NG + 2)
            dve.tensor_copy(gap2_rep, gap2[:].unsqueeze(2).to_broadcast([128, B, 128])).then_inc(S["gate_dve"], 1)
            dve.wait_ge(S["gate_pe"], 1)
            dve.tensor_scalar(fc1_out, psum[:, 0, 0:B], vec[:, 13:14], 0.0, ALU.add, ALU.max).then_inc(S["gate_dve"], 1)
            dve.wait_ge(S["gate_pe"], 3)
            dve.tensor_tensor(score_row, psum[0:B, 2, 0:C], fc2_bias, ALU.add).then_inc(S["gate_dve"], 1)
            dve.tensor_tensor(offset, psum[:, 1, 0:6 * B].rearrange("p (b t) -> p b t", t=6),
                              off_bias.unsqueeze(1).to_broadcast([128, B, 6]), ALU.add).then_inc(S["gate_dve"], 1)
            dve.wait_ge(S["gate_act"], 1)
            dve.tensor_copy(score_rep, score_row[:, 0:KS].unsqueeze(1).to_broadcast([B, 4, KS])).then_inc(S["gate_dve"], 1)
            bor = consts[0:B, _AT["batch_of_row"][0]:_AT["batch_of_row"][1]]
            dve.tensor_tensor(score_diag, score_row.unsqueeze(1).to_broadcast([B, B, C]),
                              bor.unsqueeze(2).to_broadcast([B, B, C]), ALU.mult).then_inc(S["gate_dve"], 1)
            dve.wait_ge(S["gate_pe"], 4)
            dve.tensor_copy(score_col, psum[:, 4, 0:B]).then_inc(S["gate_dve"], 1)
            dve.wait_ge(S["gate_dve"], 8)
            col = score_col.unsqueeze(2).to_broadcast([128, B, C])
            every = psum[:, 3, :].rearrange("p (b c) -> p b c", c=C)
            dve.tensor_tensor(equal, every, col, ALU.is_equal).then_inc(S["gate_dve"], 1)
            dve.tensor_tensor(greater, every, col, ALU.is_gt)
            dve.wait_ge(S["gate_dve"], 9)
            dve.tensor_tensor(equal, equal, const("earlier").unsqueeze(1).to_broadcast([128, B, C]), ALU.mult).then_inc(S["gate_dve"], 1)
            dve.wait_ge(S["gate_dve"], 10)
            dve.tensor_tensor(greater, greater, equal, ALU.add).then_inc(S["gate_dve"], 1)
            dve.wait_ge(S["gate_dve"], 11)
            dve.tensor_reduce(rank, greater, AX.X, ALU.add).then_inc(S["gate_dve"], 1)
            dve.wait_ge(S["gate_dve"], 12)
            dve.tensor_scalar(rank, rank, float(KS), None, ALU.is_lt).then_inc(S["gate_dve"], 1)
            dve.wait_ge(S["gate_act"], 4)
            dve.tensor_scalar(gain, gain, 1.0, None, ALU.add).then_inc(S["gate_dve"], 1)
            dve.wait_ge(S["gate_dve"], 14)
            n = 14
            full = [128, B, NKT]
            for m in range(len(KERNELS)):
                a = _AT["valid"][0] + m * NKT
                t = tap_w[:, m, :, :]
                for o, i0, i1, op in ((t, taps[:, m, :].unsqueeze(1).to_broadcast(full), gain[:, :, 2 * m:2 * m + 1].to_broadcast(full), ALU.mult),
                                      (t, t, shift[:, :, 2 * m + 1:2 * m + 2].to_broadcast(full), ALU.add),
                                      (live, consts[:, a:a + NKT].unsqueeze(1).to_broadcast(full), rank.unsqueeze(2).to_broadcast(full), ALU.mult),
                                      (t, t, live, ALU.mult)):
                    dve.tensor_tensor(o, i0, i1, op).then_inc(S["gate_dve"], 1)
                    n += 1
                    dve.wait_ge(S["gate_dve"], n)

            def conv_weights(b4, bh, par, count):
                b = bh * NB4 + b4
                w = conv_w[:, par, bh, :, :]
                for m in (2, 1, 0):
                    o = (TAP - KERNELS[m]) // 2
                    lo, hi = 2 * o, 2 * (TAP - o)
                    shape = [128, hi - lo, C]
                    dst = (w if m == 2 else conv_t)[:, lo:hi, :]
                    dve.tensor_tensor(dst, tap_w[:, m, b, lo:hi].unsqueeze(2).to_broadcast(shape),
                                      fuse_w[:, m, :].unsqueeze(1).to_broadcast(shape), ALU.mult).then_inc(S["dv_mulw"], 1)
                    count += 1
                    dve.wait_ge(S["dv_mulw"], count)
                    if m != 2:
                        dve.tensor_tensor(w[:, lo:hi, :], w[:, lo:hi, :], conv_t[:, lo:hi, :], ALU.add).then_inc(S["dv_mulw"], 1)
                        count += 1
                        dve.wait_ge(S["dv_mulw"], count)
                return count

            count = 0
            for b4 in range(2):
                for bh in range(2):
                    count = conv_weights(b4, bh, b4, count)
                    dve.engine_nop().then_inc(S["dv_convw"], 1)
            for b4 in range(NB4):
                for half in range(2):
                    m = 2 * b4 + half
                    dve.wait_ge(S["pe_conv"], m + 1)
                    if m >= 2:
                        dve.wait_ge(S[f"out_done{half}"], 32 * b4)
                    dve.scalar_tensor_tensor(result[:, m % 2, :], psum[:, m % 2, :], vec[:, 10:11], x2[:, m * G:(m + 1) * G],
                                             ALU.add, ALU.add).then_inc(S["dv_result"], 1)
                if b4 + 2 < NB4:
                    for bh in range(2):
                        count = conv_weights(b4 + 2, bh, b4 % 2, count)
                        dve.engine_nop().then_inc(S["dv_convw"], 1)


def _pack(sizes, parts):
    at, n = _columns(sizes)
    packed = np.zeros((128, n), np.float32)
    for name, blocks in parts.items():
        for row, column, v in blocks:
            v = v.reshape(len(v), -1)
            packed[row:row + v.shape[0], at[name][0] + column:at[name][0] + column + v.shape[1]] = v
    return packed


def _layout(inputs):
    a = {k: np.asarray(v) for k, v in inputs.items()}
    L0, L1 = "L0_conv_", "L1_conv_"
    kernels = []
    for k in KERNELS:
        o = (TAP - k) // 2
        w = np.pad(a[f"{L1}dw{k}"][:KS, 0], ((0, 0), (o, o), (o, o + 1)))
        kernels.append(w.reshape(KS, TAP, 2, 4).transpose(3, 0, 1, 2).reshape(128, NKT))
    w_qkv, w_proj, w_mlp1 = a[L0 + "w_qkv"].reshape(C, 3, C), a[L0 + "w_proj"], a[L0 + "w_mlp1"]
    halves = (0, C)
    proj_rows = [(j * 32 + hh * 16 + bh * HD, bh * C, w_proj[(4 * hh + j) * HD:(4 * hh + j + 1) * HD])
                 for j in range(4) for hh in range(2) for bh in range(2)]
    vectors = [L0 + "ln1_scale", L0 + "ln1_bias", L0 + "ln2_scale", L0 + "ln2_bias", L0 + "b_qkv", L0 + "b_proj",
               L0 + "b_mlp2", L1 + "pw1_b", L1 + "pw_b"]
    by_channel = np.concatenate([a[v].reshape(-1, C).T for v in vectors], axis=1)
    vec = [(r, 0, by_channel) for r in halves] + [(0, 11, a[L0 + "b_mlp1"].reshape(2, 128).T), (0, 13, a[L1 + "fc1_b"].reshape(128, 1))]
    table = a[L0 + "rel_bias_table"]
    return {
        "x": a["x"].reshape(B, C, PIX),
        "consts": _constants(),
        "weights": _pack(_WEIGHTS, {
            "vec": vec,
            "proj_w": proj_rows,
            "mlp2_w": [(0, 0, a[L0 + "w_mlp2"].reshape(2, 128, C).transpose(1, 0, 2))],
            "pw1_w": [(r, r, a[L1 + "pw1_w"].T) for r in halves],
            "fc1_w": [(r, 0, a[L1 + "fc1_w"].T) for r in halves],
            "fc2_w": [(0, 0, a[L1 + "fc2_w"].T)],
            "off_w": [(r, 0, a[L1 + "off_w"].T) for r in halves],
            "off_bias": [(0, 0, np.broadcast_to(a[L1 + "off_b"], (128, 6)))],
            "fc2_bias": [(0, 0, np.broadcast_to(a[L1 + "fc2_b"], (B, C)))],
            "fuse_w": [(r * KS, 0, a[L1 + "pw_w"][:, :3 * KS].reshape(C, 3, KS).transpose(2, 1, 0)) for r in range(4)],
            "taps": [(0, 0, np.stack(kernels, axis=1))],
        }),
        "raw": _pack(_RAW, {
            "qkv": [(r, i * 128 + r, w_qkv[:, i]) for r in halves for i in range(3)],
            "proj": [(r, r, w_proj) for r in halves],
            "mlp1": [(r, r // C * HIDDEN, w_mlp1) for r in halves],
        }),
        "rel_flipped": table[::-1], "rel_table": table,
    }


def kernel(**inputs):
    import concourse.bacc as _bacc
    from concourse.bass_utils import run_bass_kernel_spmd as _run

    nc = _bacc.Bacc("TRN2", target_bir_lowering=False, num_devices=1)
    arrays, args = {}, {}
    for name, v in _layout(inputs).items():
        v = np.ascontiguousarray(v)
        arrays[f"in_{name}"] = v
        args[name] = nc.dram_tensor(f"in_{name}", v.shape, mybir.dt.from_np(v.dtype), kind="ExternalInput").ap()
    out = nc.dram_tensor("out", (B, C, PIX), mybir.dt.float32, kind="ExternalOutput").ap()
    conv_seq_kernel(nc, args, out)
    r = _run(nc, [arrays], core_ids=[0])
    return r.results[0]["out"].reshape(B, C, H, W)
```

```python
import numpy as np
import concourse.bass as bass
from concourse import mybir
from contextlib import ExitStack

B, C, H, W = 8, 64, 32, 32
WS, NH, HD = 8, 8, 8
NB4 = B // 2
PIX = H * W
COLS = NB4 * PIX
G = 512
NG = COLS // G
NW = G // (WS * WS)
T = WS * WS
HIDDEN = 4 * C
KS = C // 2
KERNELS = (3, 5, 7)
TAP = 7
PAD = TAP // 2
PATCH = WS * (2 * WS - 1)
PW = W + 2 * PAD
PIMG = PW * (H + 2 * PAD)
SHIFTS = 128 // KS
NKT = (TAP + 1) // SHIFTS * TAP
SIMG = PW * (PIMG // PW - (SHIFTS - 1))
NTAP = NKT * 2
GATES = ((0, NB4 // 2), (NB4 // 2, NB4 // 2))
EPS1 = 1e-5
SCALE = float(HD) ** -0.5

_p = np.arange(128)
_bh, _c = _p // C, _p % C


def _valid():
    v = np.zeros((128, len(KERNELS), NKT, 2), np.float32)
    for i, k in enumerate(KERNELS):
        o = (TAP - k) // 2
        for shift in range(SHIFTS):
            for t in range(NKT):
                for parity in range(2):
                    dy, dx = SHIFTS * (t // TAP) + shift - parity, t % TAP
                    if o <= dy < TAP - o and o <= dx < TAP - o:
                        v[shift * KS:(shift + 1) * KS, i, t, parity] = 1
    return v.reshape(128, -1)


_CONST = {
    "center": np.where(_bh[:, None] == _bh, (_p[:, None] == _p) - 1.0 / C, 0),
    "average": np.where(_bh[:, None] == _bh, 1.0 / C, 0),
    "ident": _p[:, None] == _p,
    "reverse": (_p % T)[:, None] == T - 1 - _p % T,
    "head_of_channel": (_c // HD)[:, None] == np.arange(NH),
    "head_of_row": (_p % NH)[:, None] == np.arange(NH),
    "window_of_row": (_p // NH % NW)[:, None] == np.arange(NW),
    "same_half": _bh[:, None] == _bh,
    "ones_by_head_half": (np.arange(64) // 32 == np.arange(64) % 32 // 16)[None]
    & (_bh[:, None] == np.arange(64) % 16 // HD),
    "earlier": np.arange(C) < (_p % KS)[:, None],
    "valid": _valid(),
    "batch_of_row": _p[:, None] == np.arange(B),
}
_AT, _n = {}, 0
for _k, _v in _CONST.items():
    _AT[_k] = (_n, _n + _v.shape[1])
    _n += _v.shape[1]
NCONST = _n


_WEIGHTS = {"vec": 16, "proj_w": 128, "mlp2_w": 2 * C, "pw1_w": 128, "fc1_w": 2 * C, "fc2_w": C, "off_w": 6,
            "off_bias": 6, "fc2_bias": C, "fuse_w": 3 * C, "taps": 3 * NTAP}
_RAW = {"qkv": 3 * 128, "proj": 128, "mlp1": HIDDEN}


def _columns(sizes):
    at, n = {}, 0
    for name, size in sizes.items():
        at[name] = (n, n + size)
        n += size
    return at, n


_WAT, NWEIGHT = _columns(_WEIGHTS)
_RAT, NRAW = _columns(_RAW)


NFIRST = _AT["average"][1]


def _constants():
    return np.ascontiguousarray(np.concatenate([np.asarray(v, np.float32) for v in _CONST.values()], axis=1))


def conv_seq_kernel(nc, d, out):
    F32, F32R = mybir.dt.float32, mybir.dt.float32r
    ALU, ACT, AX = mybir.AluOpType, mybir.ActivationFunctionType, mybir.AxisListType

    ctx = ExitStack()
    with ctx:
        attention_memory = ExitStack()

        def sb(name, shape, dt=F32, stack=ctx):
            return stack.enter_context(nc.sbuf_tensor(name, shape, dt))

        def sem(name):
            return ctx.enter_context(nc.semaphore(name))

        consts = sb("consts", [128, NCONST])
        center_average = sb("center_average", [128, 2, 128], F32R)

        def const(name):
            a, b = _AT[name]
            return consts[:, a:b]

        x = sb("x", [128, COLS])
        x1 = sb("x1", [128, COLS])
        x2 = x
        weights = sb("weights", [128, NWEIGHT])

        def weight(name):
            a, b = _WAT[name]
            return weights[:, a:b]

        vec = weight("vec")
        proj_w = weight("proj_w")
        mlp2_w = weight("mlp2_w").rearrange("p (f c) -> p f c", f=2)
        pw1_w, fc1_w, fc2_w, off_w = (weight(n) for n in ("pw1_w", "fc1_w", "fc2_w", "off_w"))
        fuse_w = weight("fuse_w").rearrange("p (m c) -> p m c", c=C)
        taps = weight("taps").rearrange("p (m t) -> p m t", t=NTAP)
        fc2_bias, off_bias = weight("fc2_bias")[0:B], weight("off_bias")
        qkv_w = sb("qkv_w", [128, 3, 128])
        mlp1_w = sb("mlp1_w", [128, 2, HIDDEN], F32R)
        qkv_bias = sb("qkv_bias", [128, 3])
        q_bias = sb("q_bias", [128, 1])
        proj_bias = sb("proj_bias", [128, 1])
        mlp1_bias = sb("mlp1_bias", [128, 2])
        eps = sb("eps", [128, 1])
        rel_raw = x1[0:T, 0:2 * NH * PATCH].rearrange("p (n f h) -> p n f h", n=2, h=NH)
        square_logvar = sb("square_logvar", [128, 2, G])
        square, logvar = square_logvar[:, 0, :], square_logvar[:, 1, :]
        square_logvar2 = sb("square_logvar2", [128, 2, G])
        square2, logvar2 = square_logvar2[:, 0, :], square_logvar2[:, 1, :]
        mlp_out, relu_out = square_logvar, square_logvar2
        maxima = sb("maxima", [128, NW * NH])
        maxima_t = sb("maxima_t", [128, T])
        h_sum = sb("h_sum", [128, NG])
        r_sum = sb("r_sum", [128, NG])
        gaps = sb("gaps", [128, 2, B])
        ones8 = sb("ones8", [B, 128])

        def at(name, shape, dt=F32):
            return sb(name, shape, dt, attention_memory)

        q_heads = at("q_heads", [128, 2, NW, NH, T], F32R)
        k_blocks = at("k_blocks", [128, 2, NW, 128], F32R)
        k_heads = at("k_heads", [128, NW, NH, T], F32R)
        q_blocks = at("q_blocks", [128, NW, 128], F32R)
        pick = at("pick", [128, NW, 128], F32R)
        minus_max = at("minus_max", [128, NH, T], F32R)
        rel = at("rel", [128, 2, NH * T], F32R)
        reverse = at("reverse", [128, 128], F32R)
        probs = at("probs", [128, NW, NH * T])
        v_blocks = at("v_blocks", [128, 2, NW * NH * 32])
        q, k, normed, rstd = (at(n, [128, G]) for n in ("q", "k", "normed", "rstd"))
        attended, rstd2 = (at(n, [128, G]) for n in ("attended", "rstd2"))
        q_high = at("q_high", [128, G], F32R)
        projected = square2
        inv_sum = at("inv_sum", [128, 4 * T])
        parts = at("parts", [128, 2, G], F32R)
        normed2 = at("normed2", [128, 2, COLS], F32R)
        raw = probs[:].rearrange("p w n -> p (w n)")[:, 0:NRAW]
        qkv_raw, proj_raw, mlp1_raw = (raw[:, a:b] for a, b in _RAT.values())
        qkv_raw = qkv_raw.rearrange("p (i o) -> p i o", i=3)
        attention_memory.close()

        images = sb("images", [128, 2, NB4, PIMG], F32R)
        shifted = sb("shifted", [128, 2, 2, SIMG], F32R)
        conv_w0 = sb("conv_w0", [128, 2, NKT, 128], F32R)
        before_v = 4 * NW * NH * T + 4 * NW * 128 + 3 * NH * T + 128
        small = sb("small", [128, before_v - 2 * NB4 * PIMG - 4 * SIMG - 2 * NKT * 128])
        hidden = sb("hidden", [128, 2, 4, G])
        gate0_memory = sb("gate0_memory", [128, 1600])
        conv_w1 = sb("conv_w1", [128, 2, NKT, 128], F32R)
        conv_w = (conv_w0, conv_w1)
        whole_w = sb("whole_w", [128, 2, NKT, 128])
        product5 = sb("product5", [128, 2, 5 * 2, C])
        product3 = sb("product3", [128, 2, 3 * 2, C])

        tap_w = small[:, 0:3 * B * NTAP].rearrange("p (m b t) -> p m b t", m=3, b=B)
        ones = small[:, 3 * B * NTAP:3 * B * NTAP + 128]

        def gate_memory(space, nb):
            n, a0, out = 2 * nb, 0, {}
            for name, shape in (("off_products", (n, 6)), ("greater", (n, C)), ("equal", (n, C)), ("diag", (n, C)),
                                ("score_rep", (SHIFTS, KS)), ("live", (3, n, NTAP)), ("score_row", (C,)), ("offset", (n, 6)),
                                ("gain", (n, 6)), ("shift", (n, 6)), ("pooled", (2, nb)), ("fc1_out", (n,)), ("score_col", (n,)), ("rank", (n,))):
                size = int(np.prod(shape))
                dims = " ".join("abc"[:len(shape)])
                out[name] = space[:, a0:a0 + size].rearrange(f"p ({dims}) -> p {dims}", **dict(zip("abc", shape)))
                a0 += size
            return out

        gates = (gate_memory(gate0_memory[:], GATES[0][1]), gate_memory(x1[:], GATES[1][1]))

        psum = ctx.enter_context(nc.psum_tensor("psum", [128, 8, 512], F32))
        NORM, MISC0, MISC1, MAX0, PROB0, PV = 0, 1, 2, 3, 5, 7

        S = {n: sem(n) for n in (
            "zeroed", "eps_set", "center_in", "consts_in", "x_first", "x_rest", "qkv_in", "raw_in", "weights_in", "rel_in",
            "pe_qkv_bias", "dv_qkv_bias", "qkv_ready", "pe_biases", "weights_ready", "dv_rel_high", "rel_ready", "dv_center", "dv_scaled", "dv_high",
            "x_high", "ac_x1", "po_pick", "x_low", "square_low", "x1_low", "square2_low", "dv_whole2", "dv_high2",
            "pe_xc", "pe_var", "pe_q", "pe_k", "pe_v", "pe_max", "pe_maxt", "pe_scores", "pe_pv", "pe_proj", "pe_xc2", "pe_var2",
            "ac_sq", "ac_log", "ac_rstd", "ac_q", "ac_q_high", "ac_heads", "ac_k", "ac_v", "ac_probs", "ac_proj", "ac_sq2", "ac_log2", "ac_rstd2", 
            "dv_normed", "q_blocked", "dv_kh", "ac_kb", "dv_kb", "po_kb", "dv_q_low", "po_qh", "dv_max", "dv_maxt", "dv_minus", "dv_inv", "dv_att", "dv_x1", "dv_normed2",
            "pe_mlp1", "pe_mlp2", "pe_pw1", "ac_gelu", "ac_mlp", "ac_relu", "dv_x2", "dv_hsum", "dv_rsum",
            "po_images",
            "gate_dve", "gate_pe", "gate_act", "po_product", "dv_product", "dv_whole", "ac_high", "ac_first_high", "first_low_weights",
            "low_weights",
            "shift_in0", "shift_in1", "pe_conv", "dv_result", "out_done")}
        HIDDEN0, MLP, PW1, GATE, CONV0 = 3, 1, (7, 2), 0, 3

        def x_view(g, s):
            base = g * G + s * (G // 2)
            return x[:, bass.ds(base, G // 2)].rearrange("p (a w b) -> p w a b", a=WS, b=WS)

        def stripe(t, s):
            return t[:, s * (G // 2):(s + 1) * (G // 2)].rearrange("p (w a b) -> p w a b", a=WS, b=WS)

        def image_rows(part, n, b4, half):
            img = images[:, part, bass.ds(b4, 1), :].rearrange("p b (y x) -> p (b y) x", x=PW)
            return img[:, PAD + half * 16:PAD + half * 16 + 16, PAD:PAD + W]

        def taps_window(w, m):
            o = (TAP - KERNELS[m]) // 2
            w = w.rearrange("p (h x) (r o) -> p h (x r) o", h=NKT // TAP, r=2)
            return w[:, :, 2 * o:2 * (TAP - o), :]

        def factors(b4, bh, m):
            o = (TAP - KERNELS[m]) // 2
            shape = [128, NKT // TAP, 2 * KERNELS[m], C]
            tap = tap_w[:, m, bass.ds(2 * b4 + bh, 1), :]
            tap = tap.rearrange("p b (h x) -> p (b h) x", h=NKT // TAP)[:, :, 2 * o:2 * (TAP - o)]
            return tap.unsqueeze(3).to_broadcast(shape), fuse_w[:, m, :].unsqueeze(1).unsqueeze(1).to_broadcast(shape)

        GATE_STEPS, GATE_PE, GATE_ACT = 19, 3, 4

        def max_banks(n):
            return (MAX0, MAX0 + 1, MISC0) + ((PROB0, PROB0 + 1) if isinstance(n, int) and n == 0 else ())

        def low_part(engine, whole, high, low):
            return engine.tensor_tensor(low, whole, high.bitcast(F32), ALU.subtract)

        def low_of_x(engine, n):
            for s in range(2):
                ins = low_part(engine, x_view(n, s), stripe(parts[:, 0, :], s), stripe(parts[:, 1, :], s))
            ins.then_inc(S["x_low"], 1)

        def low_of_x1(engine, c):
            engine.wait_ge(S["ac_x1"], c + 1)
            low_part(engine, x1[:, bass.ds(c * G, G)], parts[:, 0, :], parts[:, 1, :]).then_inc(S["x1_low"], 1)

        def low_of_square2(engine, c):
            engine.wait_ge(S["ac_sq2"], c + 1)
            low_part(engine, square2, parts[:, 0, :], parts[:, 1, :]).then_inc(S["square2_low"], 1)

        def low_of_square(engine):
            low_part(engine, square, parts[:, 0, :], parts[:, 1, :]).then_inc(S["square_low"], 1)

        def q_block(copy, source):
            for bh in range(2):
                r = slice(bh * C, (bh + 1) * C)
                ins = copy(q_blocks[r, :, bh * T:(bh + 1) * T], source[r, :].rearrange("p (w t) -> p w t", t=T))
            ins.then_inc(S["q_blocked"], 1)

        def k_block_low(engine, n, bh, done):
            engine.wait_ge(S["ac_kb"], n + 1)
            r = slice(bh * C, (bh + 1) * C)
            both = k_blocks[r, :, :, bh * T:(bh + 1) * T]
            low_part(engine, k[r, :].rearrange("p (w t) -> p w t", t=T), both[:, 0], both[:, 1]).then_inc(done, 1)

        block = ctx.enter_context(nc.Block())

        @block.sync
        def _(sp):
            def load_x(b4, columns, done):
                for bh in range(2):
                    sp.dma_start(x[bh * C:(bh + 1) * C, b4 * PIX + columns.start:b4 * PIX + columns.stop],
                                 d["x"][bh * NB4 + b4, :, columns]).then_inc(done, 16)

            load_x(0, slice(0, G), S["x_first"])
            sp.dma_start(consts[:, NFIRST:], d["consts"][:, NFIRST:]).then_inc(S["consts_in"], 16)
            side = 2 * WS - 1
            run = ((WS - 1) * side + WS) * NH
            for n, name in enumerate(("rel_flipped", "rel_table")):
                src = bass.AP(d[name].tensor, d[name].offset, [[side * NH, WS], [NH, WS], [1, run]])
                sp.dma_start(rel_raw[:, n, :, :].rearrange("p f h -> p (f h)")[:, 0:run], src).then_inc(S["rel_in"], 16)
            nqkv = _RAT["qkv"][1]
            sp.dma_start(raw[:, nqkv:], d["raw"][:, nqkv:]).then_inc(S["raw_in"], 16)
            load_x(0, slice(G, PIX), S["x_rest"])
            sp.dma_start(weights[:, _WAT["vec"][1]:], d["weights"][:, _WAT["vec"][1]:]).then_inc(S["weights_in"], 16)
            for b4 in range(1, NB4):
                load_x(b4, slice(0, PIX), S["x_rest"])

            def copy_images(b4, bh):
                sp.wait_ge(S["po_images"], NB4 + 2 * b4 + 2)
                for r in range(SHIFTS):
                    src = images[bh * C:bh * C + KS, :, bass.ds(b4, 1), r * PW:r * PW + SIMG].rearrange("p l b f -> p (l b) f")
                    sp.dma_start(shifted[r * KS:(r + 1) * KS, bh, :, :].bitcast(F32), src.bitcast(F32)).then_inc(S[f"shift_in{bh}"], 16)

            def store(b4, bh):
                sp.wait_ge(S["dv_result"], 2 * b4 + bh + 1)
                sp.dma_start(out[bass.ds(bh * NB4 + b4, 1), :, :].rearrange("b c f -> (b c) f"),
                             x2[bh * C:(bh + 1) * C, bass.ds(b4 * PIX, PIX)]).then_inc(S["out_done"], 16)

            copy_images(0, 0)
            copy_images(0, 1)
            with sp.Fori(0, NB4 - 1) as i:
                for bh in range(2):
                    sp.wait_ge(S["pe_conv"], 2 * i + bh + 1)
                    copy_images(i + 1, bh)
                    store(i, bh)
            for bh in range(2):
                store(NB4 - 1, bh)
            sp.wait_ge(S["out_done"], 16 * B)

        @block.gpsimd
        def _(pool):
            for t in (q_blocks[:].bitcast(F32), v_blocks[:], k_blocks[:].bitcast(F32), gaps[:]):
                pool.memset(t, 0.0).then_inc(S["zeroed"], 1)
            pool.memset(ones8[:], 1.0).then_inc(S["zeroed"], 1)

            def q_head(n, s, part):
                if not (isinstance(n, int) and n == 0):
                    pool.wait_ge(S["pe_scores"], NW * (n - 1) + 2 * s + 2)
                pool.wait_ge(*((S["ac_q_high"], n + 1) if part == 0 else (S["dv_q_low"], n + 1)))
                shape = [128, NW // 4, NH, T]
                r = slice(s * NW // 4, (s + 1) * NW // 4)
                some = (q_high, q)[part][:].bitcast(F32).rearrange("p (w t) -> p w t", t=T)[:, r]
                ins = pool.tensor_tensor(q_heads[:, part, r], some.unsqueeze(2).to_broadcast(shape),
                                         const("head_of_channel").unsqueeze(1).unsqueeze(3).to_broadcast(shape), ALU.mult)
                if part == 1:
                    ins.then_inc(S["po_qh"], 1)

            def half_of_k_block(n, before):
                pool.wait_ge(S["po_qh"], before)
                k_block_low(pool, n, 1, S["po_kb"])
                pool.wait_ge(S["po_kb"], n)

            def step(g, nxt, prev):
                if nxt is not None:
                    pool.wait_ge(S["x_high"], nxt + 1)
                    low_of_x(pool, nxt)
                if isinstance(g, int) and g == 0:
                    for part in range(2):
                        q_head(g, 1, part)
                else:
                    if nxt is not None:
                        pool.wait_ge(S["x_low"], nxt + 1)
                    half_of_k_block(g, 4 * g + 2)
                if nxt is not None:
                    pool.wait_ge(S["ac_sq"], nxt + 1)
                    low_of_square(pool)
                q_head(g, 2, 1)
                q_head(g, 3, 1)
                if prev is not None:
                    low_of_x1(pool, prev)
                if nxt is not None:
                    q_head(nxt, 0, 0)
                    q_head(nxt, 0, 1)
                if prev is not None:
                    low_of_square2(pool, prev)
                if nxt is not None:
                    q_head(nxt, 1, 0)
                    q_head(nxt, 1, 1)

            pool.wait_ge(S["consts_in"], 16)
            pool.tensor_tensor(pick[:], const("window_of_row").unsqueeze(2).to_broadcast([128, NW, 128]),
                               const("same_half").unsqueeze(1).to_broadcast([128, NW, 128]), ALU.mult).then_inc(S["po_pick"], 1)
            for part in range(2):
                q_head(0, 0, part)
            step(0, 1, None)
            with pool.Fori(0, NG // 2 - 1) as i:
                step(2 * i + 1, 2 * i + 2, 2 * i)
                step(2 * i + 2, 2 * i + 3, 2 * i + 1)
            step(NG - 1, None, NG - 2)

            pool.wait_ge(S["pe_scores"], NW * NG)
            for b4 in range(NB4):
                for part in range(2):
                    ins = pool.memset(images[:, part, b4, :].bitcast(F32), 0.0)
                ins.then_inc(S["po_images"], 1)
            pool.wait_ge(S["pe_pv"], 2 * NG)
            pool.memset(ones, 1.0).then_inc(S["zeroed"], 1)

            def low_image(n, b4, half):
                pool.wait_ge(S["ac_relu"], n + 1)
                pool.tensor_tensor(image_rows(1, n, b4, half), relu_out[:, half, :].rearrange("p (y x) -> p y x", x=W),
                                   image_rows(0, n, b4, half).bitcast(F32), ALU.subtract).then_inc(S["po_images"], 1)

            def products(b4, bh):
                u = 2 * b4 + bh
                if u >= 2:
                    pool.wait_ge(S["low_weights"], u - 1)
                pool.tensor_tensor(taps_window(whole_w[:, bh], 2), *factors(b4, bh, 2), ALU.mult).then_inc(S["po_product"], 1)
                if u > 0:
                    pool.wait_ge(S["dv_whole"], u)
                pool.tensor_tensor(product3[:], *factors(b4, bh, 0), ALU.mult).then_inc(S["po_product"], 1)

            def low_weights(b4, bh):
                pool.wait_ge(S["ac_high"], 2 * b4 + bh + 1)
                pool.tensor_tensor(conv_w[bh][:, 1], whole_w[:, bh], conv_w[bh][:, 0].bitcast(F32), ALU.subtract
                                   ).then_inc(S["low_weights"], 1)

            with pool.Fori(0, NB4 - 2) as b4:
                for half in range(2):
                    low_image(2 * b4 + half, b4, half)
            low_image(NG - 4, NB4 - 2, 0)
            pool.wait_ge(S["gate_dve"], GATE_STEPS)
            pool.wait_ge(S["pe_mlp1"], 4 * NG)
            products(0, 0)
            low_image(NG - 3, NB4 - 2, 1)
            products(0, 1)
            low_image(NG - 2, NB4 - 1, 0)
            low_image(NG - 1, NB4 - 1, 1)
            products(1, 0)
            low_weights(0, 1)
            products(1, 1)
            low_weights(1, 0)
            low_weights(1, 1)
            pool.wait_ge(S["gate_dve"], 2 * GATE_STEPS)
            for b4 in range(2, NB4):
                for bh in range(2):
                    products(b4, bh)

        NBLOCKS, NZERO = 3, 6

        @block.scalar
        def _(act):
            act.dma_start(consts[:, 0:NFIRST], d["consts"][:, 0:NFIRST]).then_inc(S["center_in"], 16)
            act.dma_start(vec, d["weights"][:, 0:_WAT["vec"][1]]).then_inc(S["qkv_in"], 16)
            nqkv = _RAT["qkv"][1]
            act.dma_start(raw[:, 0:nqkv], d["raw"][:, 0:nqkv]).then_inc(S["qkv_in"], 16)
            def load_tables(which):
                act.add_instruction(mybir.InstLoadActFuncSet(name=nc.get_next_instruction_name(),
                                                             engine=mybir.EngineType.Activation, act_func_set_id=which))

            LN_AND_EXP, GELU = 6, 10
            load_tables(LN_AND_EXP)

            def high_of_x(n):
                for s in range(2):
                    ins = act.copy(stripe(parts[:, 0, :], s), x_view(n, s))
                ins.then_inc(S["x_high"], 1)

            def square_of_centered(n):
                act.wait_ge(S["pe_xc"], n + 1)
                act.activation(parts[:, 0, :], psum[:, NORM, :], ACT.Square)
                act.activation(square, psum[:, NORM, :], ACT.Square).then_inc(S["ac_sq"], 1)

            def inverse_deviation(n):
                act.wait_ge(S["pe_var"], n + 1)
                act.activation(logvar, psum[:, MISC0, :], ACT.Ln, bias=eps[:, 0:1]).then_inc(S["ac_log"], 1)
                act.wait_ge(S["ac_log"], n + 1)
                act.activation(rstd[:], logvar, ACT.Exp, scale=-0.5).then_inc(S["ac_rstd"], 1)

            def evacuate_q_and_k(n):
                act.wait_ge(S["pe_k"], n + 1)
                act.activation(k[:], psum[:, MISC1, :], ACT.Identity, bias=qkv_bias[:, 1:2]).then_inc(S["ac_k"], 1)
                act.wait_ge(S["pe_q"], n + 1)
                if not (isinstance(n, int) and n == 0):
                    act.wait_ge(S["po_qh"], 4 * n)
                act.activation(q[:], psum[:, MISC0, :], ACT.Identity, bias=q_bias[:, 0:1], scale=SCALE).then_inc(S["ac_q"], 1)
                act.activation(q_high[:], psum[:, MISC0, :], ACT.Identity, bias=q_bias[:, 0:1], scale=SCALE).then_inc(S["ac_q_high"], 1)

            def k_block_high(n):
                if not (isinstance(n, int) and n == 0):
                    act.wait_ge(S["pe_scores"], NW * n)
                act.wait_ge(S["ac_k"], n + 1)
                for bh in range(2):
                    r = slice(bh * C, (bh + 1) * C)
                    ins = act.copy(k_blocks[r, 0, :, bh * T:(bh + 1) * T], k[r, :].rearrange("p (w t) -> p w t", t=T))
                ins.then_inc(S["ac_kb"], 1)

            def evacuate_v(n, par):
                act.wait_ge(S["pe_v"], n + 1)
                vb = v_blocks[:, par, :].rearrange("p (w two h e) -> p w two h e", two=2, h=NH, e=32)
                vp = psum[:, MAX0 + 1, :].rearrange("p (w b h e) -> p w b h e", b=2, h=NH, e=HD)
                for odd in range(2):
                    for bh in range(2):
                        act.copy(vb[bh * C:(bh + 1) * C, :, odd, :, bh * HD:(bh + 1) * HD],
                                 vp[odd * T:(odd + 1) * T, :, bh, :, :]).then_inc(S["ac_v"], 1)

            def high_heads(g):
                act.wait_ge(S["ac_q_high"], g + 1)
                if not (isinstance(g, int) and g == 0):
                    act.wait_ge(S["pe_scores"], NW * g)
                some = q_high[:].bitcast(F32).rearrange("p (w t) -> p w t", t=T)[:, NW // 2:]
                for h in range(NH):
                    a = _AT["head_of_channel"][0] + h
                    ins = act.activation(q_heads[:, 0, NW // 2:, h, :], some, ACT.Identity, scale=consts[:, a:a + 1])
                ins.then_inc(S["ac_heads"], 1)

            def exponentials(g, w):
                act.wait_ge(S["pe_scores"], NW * g + w + 1)
                act.activation(probs[:, w, :], psum[:, PROB0 + w % 2, :], ACT.Exp).then_inc(S["ac_probs"], 1)

            def evacuate_projection(c):
                act.wait_ge(S["pe_proj"], c + 1)
                act.activation(projected[:], psum[:, MISC1, :], ACT.Identity, bias=proj_bias[:, 0:1]).then_inc(S["ac_proj"], 1)

            def high_of_x1(c):
                act.wait_ge(S["dv_x1"], c + 1)
                act.copy(parts[:, 0, :], x1[:, bass.ds(c * G, G)]).then_inc(S["ac_x1"], 1)

            def square_of_centered2(c):
                act.wait_ge(S["pe_xc2"], c + 1)
                act.activation(parts[:, 0, :], psum[:, NORM, :], ACT.Square)
                act.activation(square2, psum[:, NORM, :], ACT.Square).then_inc(S["ac_sq2"], 1)

            def inverse_deviation2(c):
                act.wait_ge(S["pe_var2"], c + 1)
                act.activation(logvar2, psum[:, MISC1, :], ACT.Ln, bias=eps[:, 0:1]).then_inc(S["ac_log2"], 1)
                act.wait_ge(S["ac_log2"], c + 1)
                if not (isinstance(c, int) and c == 0):
                    act.wait_ge(S["dv_normed2"], 2 * c)
                act.activation(rstd2[:], logvar2, ACT.Exp, scale=-0.5).then_inc(S["ac_rstd2"], 1)

            def step(g, nxt, prev, par):
                if nxt is not None:
                    high_of_x(nxt)
                if prev is not None:
                    k_block_high(g)
                high_heads(g)
                if nxt is not None:
                    square_of_centered(nxt)
                exponentials(g, 0)
                exponentials(g, 1)
                if nxt is not None:
                    inverse_deviation(nxt)
                exponentials(g, 2)
                if prev is not None:
                    evacuate_projection(prev)
                exponentials(g, 3)
                if nxt is not None:
                    evacuate_q_and_k(nxt)
                if prev is not None:
                    high_of_x1(prev)
                if nxt is not None:
                    act.wait_ge(S["ac_q_high"], nxt + 1)
                    q_block(act.copy, q_high[:].bitcast(F32))
                    evacuate_v(nxt, 1 - par)
                exponentials(g, 4)
                if prev is not None:
                    square_of_centered2(prev)
                exponentials(g, 5)
                exponentials(g, 6)
                if prev is not None:
                    inverse_deviation2(prev)
                exponentials(g, 7)

            square_of_centered(0)
            act.wait_ge(S["eps_set"], 1)
            inverse_deviation(0)
            act.wait_ge(S["qkv_ready"], 1)
            act.wait_ge(S["zeroed"], NBLOCKS)
            evacuate_q_and_k(0)
            k_block_high(0)
            evacuate_v(0, 0)
            act.wait_ge(S["x_rest"], 32 * NB4)
            act.wait_ge(S["weights_ready"], 1)
            step(0, 1, None, 0)
            with act.Fori(0, NG // 2 - 1) as i:
                step(2 * i + 1, 2 * i + 2, 2 * i, 1)
                step(2 * i + 2, 2 * i + 3, 2 * i + 1, 0)
            step(NG - 1, None, NG - 2, 1)

            def gelu(n, par, blocks=range(4)):
                for m in blocks:
                    act.wait_ge(S["pe_mlp1"], 4 * n + m + 1)
                    act.activation(hidden[:, par, m, :], psum[:, HIDDEN0 + m, :], ACT.Gelu,
                                   bias=mlp1_bias[:, m % 2:m % 2 + 1]).then_inc(S["ac_gelu"], 1)

            def evacuate_mlp(n, par):
                act.wait_ge(S["pe_mlp2"], n + 1)
                act.activation(mlp_out[:, par, :], psum[:, MLP, :], ACT.Identity, bias=vec[:, 8:9]).then_inc(S["ac_mlp"], 1)

            def relu(n, b4, half):
                act.wait_ge(S["pe_pw1"], n + 1)
                act.wait_ge(S["po_images"], n + NB4 - 1)
                bank = psum[:, PW1[half], :]
                act.activation(relu_out[:, half, :], bank, ACT.Relu, bias=vec[:, 9:10])
                act.activation(image_rows(0, n, b4, half), bank.rearrange("p (y x) -> p y x", x=W), ACT.Relu,
                               bias=vec[:, 9:10]).then_inc(S["ac_relu"], 1)

            def gate(k):
                mem, n = gates[k], 2 * GATES[k][1]
                row = mem["score_row"][0:n]
                act.wait_ge(S["gate_dve"], k * GATE_STEPS + 5)
                act.activation(row, row, ACT.Sigmoid).then_inc(S["gate_act"], 1)
                act.wait_ge(S["gate_dve"], k * GATE_STEPS + 6)
                act.activation(mem["offset"], mem["offset"], ACT.Tanh).then_inc(S["gate_act"], 1)
                act.wait_ge(S["gate_act"], k * GATE_ACT + 2)
                act.activation(mem["gain"], mem["offset"], ACT.Sigmoid).then_inc(S["gate_act"], 1)
                act.activation(mem["shift"], mem["offset"], ACT.Tanh).then_inc(S["gate_act"], 1)

            def high_weights(u, bh):
                act.wait_ge(S["dv_whole"], u + 1)
                if not (isinstance(u, int) and u < 2):
                    act.wait_ge(S["pe_conv"], u - 1)
                if isinstance(u, int) and u == 0:
                    act.copy(conv_w[bh][:, 0, 0:TAP], whole_w[:, bh, 0:TAP]).then_inc(S["ac_first_high"], 1)
                    act.copy(conv_w[bh][:, 0, TAP:], whole_w[:, bh, TAP:]).then_inc(S["ac_high"], 1)
                else:
                    act.copy(conv_w[bh][:, 0], whole_w[:, bh]).then_inc(S["ac_high"], 1)

            gelu(0, 0)
            act.wait_ge(S["pe_pv"], 2 * NG)
            gelu(1, 1, range(0, 2))
            evacuate_projection(NG - 1)
            gelu(1, 1, range(2, 4))
            high_of_x1(NG - 1)
            evacuate_mlp(0, 0)
            square_of_centered2(NG - 1)
            load_tables(LN_AND_EXP)
            inverse_deviation2(NG - 1)
            load_tables(GELU)
            with act.Fori(0, NG // 2 - 2) as i:
                gelu(2 * i + 2, 0)
                evacuate_mlp(2 * i + 1, 1)
                relu(2 * i, i, 0)
                gelu(2 * i + 3, 1)
                evacuate_mlp(2 * i + 2, 0)
                relu(2 * i + 1, i, 1)
            gelu(NG - 2, 0)
            evacuate_mlp(NG - 3, 1)
            gate(0)
            relu(NG - 4, NB4 - 2, 0)
            gelu(NG - 1, 1)
            evacuate_mlp(NG - 2, 0)
            relu(NG - 3, NB4 - 2, 1)
            evacuate_mlp(NG - 1, 1)
            relu(NG - 2, NB4 - 1, 0)
            high_weights(0, 0)
            relu(NG - 1, NB4 - 1, 1)
            high_weights(1, 1)
            gate(1)
            with act.Fori(1, NB4) as b4:
                for bh in range(2):
                    high_weights(2 * b4 + bh, bh)

        @block.tensor
        def _(pe):
            def over_channels(bank, which):
                for part in range(2):
                    ins = pe.matmul(psum[:, bank, :], center_average[:, which, :], parts[:, part, :], start=part == 0, stop=part == 1)
                return ins

            def centered(n):
                pe.wait_ge(S["x_low"], n + 1)
                over_channels(NORM, 0).then_inc(S["pe_xc"], 1)

            def variance(n, first=False):
                pe.wait_ge(S["square_low"], n + 1)
                if not first:
                    pe.wait_ge(S["dv_maxt"], n)
                over_channels(MISC0, 1).then_inc(S["pe_var"], 1)

            def qkv(n, first=False, second=False):
                pe.wait_ge(S["dv_normed"], n + 1)
                if not (first or second):
                    pe.wait_ge(S["ac_proj"], n - 1)
                pe.matmul(psum[:, MISC1, :], qkv_w[:, 1, :], normed[:], start=True, stop=True).then_inc(S["pe_k"], 1)
                pe.matmul(psum[:, MISC0, :], qkv_w[:, 0, :], normed[:], start=True, stop=True).then_inc(S["pe_q"], 1)
                if not first:
                    pe.wait_ge(S["dv_max"], NW * n)
                for m in range(4):
                    ins = pe.matmul(psum[:, MAX0 + 1, m * 128:(m + 1) * 128], normed[:, m * 128:(m + 1) * 128],
                                    qkv_w[:, 2, :], start=True, stop=True)
                ins.then_inc(S["pe_v"], 1)

            def scores_for_max(n, w):
                if w == 0:
                    pe.wait_ge(S["q_blocked"], n + 1)
                    pe.wait_ge(S["dv_kh"], n + 1)
                if w == 1:
                    pe.wait_ge(S["ac_v"], 4 * (n + 1))
                if w == 2:
                    pe.wait_ge(S["ac_q_high"], n + 1)
                banks = max_banks(n)
                if w >= len(banks):
                    pe.wait_ge(S["dv_max"], NW * n + w + 1 - len(banks))
                bank = psum[:, banks[w % len(banks)], :]
                pe.matmul(bank, q_blocks[:, w, :], k_heads[:, w, :, :], start=True, stop=False)
                pe.matmul(bank, reverse[:], rel[:, 0, :], start=False, stop=True).then_inc(S["pe_max"], 1)

            def transpose_maxima(n):
                pe.wait_ge(S["dv_max"], NW * (n + 1))
                pe.matmul(psum[0:C, MISC0, 0:128], maxima[:], const("ident"), start=True, stop=True).then_inc(S["pe_maxt"], 1)

            def scores(g, w):
                if w == 0:
                    pe.wait_ge(S["dv_kb"], g + 2)
                    if not (isinstance(g, int) and g == 0):
                        pe.wait_ge(S["po_kb"], g)
                    pe.wait_ge(S["dv_minus"], g + 1)
                if not (isinstance(g, int) and NW * g + w < 2):
                    pe.wait_ge(S["ac_probs"], NW * g + w - 1)
                if w == NW // 2:
                    pe.wait_ge(S["ac_heads"], g + 1)
                if w % 2 == 0:
                    pe.wait_ge(S["po_qh"], 4 * g + w // 2 + 1)
                bank = psum[:, PROB0 + w % 2, :]
                for k_part, q_part in ((0, 0), (0, 1), (1, 0)):
                    pe.matmul(bank, k_blocks[:, k_part, w, :], q_heads[:, q_part, w, :, :], start=k_part + q_part == 0, stop=False)
                pe.matmul(bank, reverse[:], rel[:, 1, :], start=False, stop=False)
                pe.matmul(bank, pick[:, w, :], minus_max[:, :, :], start=False, stop=True).then_inc(S["pe_scores"], 1)

            def weighted_values(g, quad, par, between=None):
                pe.wait_ge(S["ac_probs"], NW * g + 4 * quad + 4)
                if not (isinstance(g, int) and g == 0 and quad == 0):
                    pe.wait_ge(S["dv_att"], 2 * g + quad)
                for j in range(4):
                    for hh in range(2):
                        for p in range(4):
                            w, head = 4 * quad + p, 4 * hh + j
                            at = (w * NH + head) * 32 - 16 * hh
                            pe.matmul(psum[32 * p:32 * p + 32, PV, j * T:(j + 1) * T], v_blocks[:, par, at:at + 32],
                                      probs[:, w, head * T:(head + 1) * T], start=hh == 0, stop=hh == 1)
                    if between is not None:
                        between(j)

            def sums(quad):
                for hh in range(2):
                    for p in range(4):
                        w = 4 * quad + p
                        a = _AT["ones_by_head_half"][0] + 32 * hh
                        ins = pe.matmul(psum[32 * p:32 * p + 32, PV, 256:512], consts[:, a:a + 32],
                                        probs[:, w, hh * 256:(hh + 1) * 256], start=hh == 0, stop=hh == 1)
                ins.then_inc(S["pe_pv"], 1)

            def projection(c):
                pe.wait_ge(S["dv_att"], 2 * (c + 1))
                pe.matmul(psum[:, MISC1, :], proj_w, attended[:], start=True, stop=True).then_inc(S["pe_proj"], 1)

            def centered2(c):
                pe.wait_ge(S["x1_low"], c + 1)
                over_channels(NORM, 0).then_inc(S["pe_xc2"], 1)

            def variance2(c):
                pe.wait_ge(S["square2_low"], c + 1)
                if not (isinstance(c, int) and c >= NG - 2):
                    pe.wait_ge(S["ac_k"], c + 3)
                else:
                    pe.wait_ge(S["ac_proj"], c + 1)
                over_channels(MISC1, 1).then_inc(S["pe_var2"], 1)

            def other_maxima(n, j):
                for w in ((6,), (7,), (), ())[j]:
                    scores_for_max(n, w)
                if j == 3:
                    transpose_maxima(n)

            def step(g, nxt, prev, par):
                if nxt is not None:
                    centered(nxt)
                if prev is not None:
                    sums(1)
                scores(g, 0)
                scores(g, 1)
                if nxt is not None:
                    variance(nxt)
                scores(g, 2)
                if prev is not None:
                    projection(prev)
                scores(g, 3)
                if nxt is not None:
                    qkv(nxt, second=isinstance(nxt, int) and nxt == 1)
                scores(g, 4)
                weighted_values(g, 0, par, None if nxt is None else lambda j: scores_for_max(nxt, 0) if j == 3 else None)
                sums(0)
                if prev is not None:
                    centered2(prev)
                scores(g, 5)
                if nxt is not None:
                    scores_for_max(nxt, 1)
                scores(g, 6)
                if nxt is not None:
                    scores_for_max(nxt, 2)
                if prev is not None:
                    variance2(prev)
                if nxt is not None:
                    scores_for_max(nxt, 3)
                scores(g, 7)
                if nxt is not None:
                    for w in range(4, 6):
                        scores_for_max(nxt, w)
                weighted_values(g, 1, par, None if nxt is None else lambda j: other_maxima(nxt, j))

            pe.wait_ge(S["dv_center"], 1)
            centered(0)
            pe.wait_ge(S["qkv_in"], 32)
            for m in range(3):
                ins = pe.matmul(psum[:, PV, m:m + 1], qkv_raw[:, m, :], vec[:, 1:2], start=True, stop=True)
            ins.then_inc(S["pe_qkv_bias"], 1)
            variance(0, first=True)
            pe.wait_ge(S["qkv_ready"], 1)
            pe.wait_ge(S["raw_in"], 16)
            for f in range(2):
                pe.matmul(psum[:, PV, 3 + f:4 + f], mlp1_raw[0:C, f * 128:(f + 1) * 128], vec[0:C, 3:4], start=True, stop=True)
            pe.matmul(psum[:, PV, 5:6], proj_raw, qkv_bias[:, 2:3], start=True, stop=True).then_inc(S["pe_biases"], 1)
            qkv(0, first=True)
            pe.wait_ge(S["rel_ready"], 1)
            for w in range(NW):
                scores_for_max(0, w)
            transpose_maxima(0)
            pe.wait_ge(S["po_pick"], 1)
            pe.wait_ge(S["weights_in"], 16)
            pe.wait_ge(S["weights_ready"], 1)
            pe.wait_ge(S["x_rest"], 32 * NB4)
            step(0, 1, None, 0)
            with pe.Fori(0, NG // 2 - 1) as i:
                step(2 * i + 1, 2 * i + 2, 2 * i, 1)
                step(2 * i + 2, 2 * i + 3, 2 * i + 1, 0)
            step(NG - 1, None, NG - 2, 1)
            sums(1)

            def mlp1(n, blocks=range(4)):
                pe.wait_ge(S["dv_normed2"], 2 * n + 2)
                for m in blocks:
                    bh, f = m // 2, m % 2
                    if not (isinstance(n, int) and n == 0):
                        pe.wait_ge(S["ac_gelu"], 4 * n + m - 3)
                    for part in range(2):
                        ins = pe.matmul(psum[:, HIDDEN0 + m, :], mlp1_w[:, part, f * 128:(f + 1) * 128],
                                        normed2[:, bh, bass.ds(n * G, G)], start=part == 0, stop=part == 1)
                    ins.then_inc(S["pe_mlp1"], 1)

            def mlp2(n, par):
                if not (isinstance(n, int) and n == 0):
                    pe.wait_ge(S["ac_mlp"], n)
                for f in range(2):
                    for bh in range(2):
                        if f == 0:
                            pe.wait_ge(S["ac_gelu"], 4 * n + 2 * bh + 2)
                        ins = pe.matmul(psum[bh * C:(bh + 1) * C, MLP, :], mlp2_w[:, f, :], hidden[:, par, 2 * bh + f, :],
                                        start=f == 0, stop=f == 1)
                ins.then_inc(S["pe_mlp2"], 1)

            def pointwise1(n, half):
                pe.wait_ge(S["dv_x2"], 2 * (n + 1))
                pe.matmul(psum[:, PW1[half], :], pw1_w, x2[:, bass.ds(n * G, G)], start=True, stop=True).then_inc(S["pe_pw1"], 1)

            def gate_means(k):
                mem, n = gates[k], 2 * GATES[k][1]
                pe.wait_ge(S["gate_dve"], k * GATE_STEPS + 3)
                pe.matmul(psum[:, GATE, 8:8 + 6 * n], ones, mem["off_products"].rearrange("p b t -> p (b t)"), start=True, stop=True)
                pe.matmul(psum[:, GATE, 0:n], fc1_w, gaps[:, 0, 2 * GATES[k][0]:2 * GATES[k][0] + n], start=True,
                          stop=True).then_inc(S["gate_pe"], 1)

            def gate_scores(k):
                mem, n = gates[k], 2 * GATES[k][1]
                pe.wait_ge(S["gate_dve"], k * GATE_STEPS + 4)
                pe.matmul(psum[0:n, GATE, 64:64 + C], mem["fc1_out"], fc2_w, start=True, stop=True).then_inc(S["gate_pe"], 1)

            def gate_spread(k):
                mem, n = gates[k], 2 * GATES[k][1]
                a = _AT["batch_of_row"][0]
                pe.wait_ge(S["gate_dve"], k * GATE_STEPS + 8)
                pe.matmul(psum[:, GATE, 128:128 + n * C], ones8[0:n, :], mem["diag"][0:n], start=True, stop=True)
                pe.matmul(psum[:, GATE, 0:n], mem["score_rep"][0:n], consts[0:n, a:a + n], start=True, stop=True).then_inc(S["gate_pe"], 1)

            mlp1(0)
            mlp1(1, range(0, 2))
            projection(NG - 1)
            mlp1(1, range(2, 4))
            mlp2(0, 0)
            centered2(NG - 1)
            variance2(NG - 1)
            with pe.Fori(0, NG // 2 - 2) as i:
                mlp1(2 * i + 2)
                mlp2(2 * i + 1, 1)
                pointwise1(2 * i, 0)
                mlp1(2 * i + 3)
                mlp2(2 * i + 2, 0)
                pointwise1(2 * i + 1, 1)
            mlp1(NG - 2)
            mlp2(NG - 3, 1)
            gate_means(0)
            gate_scores(0)
            pointwise1(NG - 4, 0)
            mlp1(NG - 1, range(0, 2))
            gate_spread(0)
            mlp1(NG - 1, range(2, 4))
            mlp2(NG - 2, 0)
            pointwise1(NG - 3, 1)
            mlp2(NG - 1, 1)
            pointwise1(NG - 2, 0)
            pointwise1(NG - 1, 1)

            def convolve(b4, bh, tiles=range(NKT)):
                u = 2 * b4 + bh
                first = isinstance(b4, int) and u == 0
                if tiles[0] == 0:
                    pe.wait_ge(*((S["first_low_weights"], 1) if first else (S["low_weights"], u + 1)))
                    pe.wait_ge(S[f"shift_in{bh}"], 16 * SHIFTS * (b4 + 1))
                    if not (isinstance(b4, int) and b4 == 0):
                        pe.wait_ge(S["dv_result"], u - 1)
                for t in tiles:
                    if first and t == TAP:
                        pe.wait_ge(S["low_weights"], 1)
                    y, x0 = t // TAP * SHIFTS, t % TAP
                    for w_part, part in ((0, 0), (0, 1), (1, 0)):
                        img = shifted[:, bh, part, :].rearrange("p (y x) -> p y x", x=PW)
                        ins = pe.matmul(psum[:, CONV0 + bh, :], conv_w[bh][:, w_part, t, :], img[:, y:y + H - 1:2, x0:x0 + W],
                                        start=t == 0 and w_part + part == 0, stop=t == NKT - 1 and w_part == 1)
                if tiles[-1] == NKT - 1:
                    ins.then_inc(S["pe_conv"], 1)

            convolve(0, 0, range(0, 12))
            gate_means(1)
            convolve(0, 0, range(12, NKT))
            gate_scores(1)
            convolve(0, 1, range(0, 7))
            gate_spread(1)
            convolve(0, 1, range(7, NKT))
            with pe.Fori(1, NB4) as b4:
                for bh in range(2):
                    convolve(b4, bh)

        @block.vector
        def _(dve):
            dve.memset(eps[:], EPS1).then_inc(S["eps_set"], 1)
            dve.wait_ge(S["center_in"], 16)
            dve.tensor_copy(center_average[:].rearrange("p m c -> p (m c)"), consts[:, 0:NFIRST]).then_inc(S["dv_center"], 1)
            dve.wait_ge(S["x_first"], 32)
            for s in range(2):
                ins = dve.tensor_copy(stripe(parts[:, 0, :], s), x_view(0, s))
            ins.then_inc(S["x_high"], 1)
            dve.wait_ge(S["x_high"], 1)
            low_of_x(dve, 0)
            dve.wait_ge(S["qkv_in"], 32)
            dve.tensor_scalar(qkv_w[:], qkv_raw, vec[:, 0:1], None, ALU.mult)
            dve.wait_ge(S["pe_qkv_bias"], 1)
            dve.tensor_tensor(qkv_bias[:], psum[:, PV, 0:3], vec[:, 4:7], ALU.add).then_inc(S["dv_qkv_bias"], 1)
            dve.wait_ge(S["dv_qkv_bias"], 1)
            dve.tensor_scalar(q_bias[:], qkv_bias[:, 0:1], SCALE, None, ALU.mult).then_inc(S["qkv_ready"], 1)

            def other_weights():
                dve.wait_ge(S["raw_in"], 16)
                dve.wait_ge(S["pe_biases"], 1)
                dve.tensor_scalar(mlp1_raw, mlp1_raw, vec[:, 2:3], None, ALU.mult).then_inc(S["dv_scaled"], 1)
                dve.wait_ge(S["dv_scaled"], 1)
                dve.tensor_copy(mlp1_w[:, 0, :], mlp1_raw).then_inc(S["dv_high"], 1)
                dve.wait_ge(S["dv_high"], 1)
                low_part(dve, mlp1_raw, mlp1_w[:, 0, :], mlp1_w[:, 1, :])
                dve.tensor_tensor(mlp1_bias[:], psum[:, PV, 3:5], vec[:, 11:13], ALU.add)
                dve.tensor_tensor(proj_bias[:], psum[:, PV, 5:6], vec[:, 7:8], ALU.add).then_inc(S["weights_ready"], 1)

            def patches(n):
                return rel_raw[:, n, :, :].rearrange("p (a b) h -> p h a b", a=WS)[:, :, :, 0:WS]

            def split_bias():
                dve.wait_ge(S["rel_in"], 32)
                dve.wait_ge(S["consts_in"], 16)
                for n in range(2):
                    ins = dve.tensor_copy(rel[0:T, n, :].rearrange("p (h a b) -> p h a b", h=NH, a=WS), patches(n))
                ins.then_inc(S["dv_rel_high"], 1)
                dve.tensor_copy(reverse[:], const("reverse"))
                dve.wait_ge(S["dv_rel_high"], 1)
                for n in range(2):
                    high = rel[0:T, n, :].bitcast(F32).rearrange("p (h a b) -> p h a b", h=NH, a=WS)
                    ins = dve.tensor_tensor(rel[T:128, n, :].rearrange("p (h a b) -> p h a b", h=NH, a=WS),
                                            patches(n), high, ALU.subtract)
                ins.then_inc(S["rel_ready"], 1)

            def normalise(n):
                dve.wait_ge(S["ac_rstd"], n + 1)
                dve.tensor_tensor(normed[:], psum[:, NORM, :], rstd[:], ALU.mult).then_inc(S["dv_normed"], 1)

            def k_head(n):
                dve.wait_ge(S["ac_k"], n + 1)
                for h in range(NH):
                    a = _AT["head_of_channel"][0] + h
                    ins = dve.tensor_scalar(k_heads[:, :, h, :], k[:].rearrange("p (w t) -> p w t", t=T),
                                            consts[:, a:a + 1], None, ALU.mult)
                ins.then_inc(S["dv_kh"], 1)

            def q_low(n):
                dve.wait_ge(S["ac_q_high"], n + 1)
                if isinstance(n, int) and n == 0:
                    dve.wait_ge(S["q_blocked"], 1)
                low_part(dve, q[:], q_high[:], q[:]).then_inc(S["dv_q_low"], 1)

            def take_maximum(n, w):
                dve.wait_ge(S["pe_max"], NW * n + w + 1)
                dve.tensor_reduce(maxima[:, w * NH:(w + 1) * NH], psum[:, max_banks(n)[w % len(max_banks(n))], :].rearrange("p (h t) -> p h t", t=T),
                                  AX.X, ALU.max).then_inc(S["dv_max"], 1)

            def spread_maxima(n):
                dve.wait_ge(S["pe_maxt"], n + 1)
                dve.tensor_scalar(maxima_t[0:C, :], psum[0:C, MISC0, 0:T], -1.0, None, ALU.mult)
                dve.tensor_scalar(maxima_t[C:128, :], psum[0:C, MISC0, T:2 * T], -1.0, None, ALU.mult).then_inc(S["dv_maxt"], 1)
                dve.wait_ge(S["dv_maxt"], n + 1)
                dve.tensor_tensor(minus_max[:], maxima_t[:].unsqueeze(1).to_broadcast([128, NH, T]),
                                  const("head_of_row").unsqueeze(2).to_broadcast([128, NH, T]), ALU.mult).then_inc(S["dv_minus"], 1)

            def divide_by_sums(g, quad):
                dve.wait_ge(S["pe_pv"], 2 * g + quad + 1)
                dve.reciprocal(inv_sum[:], psum[:, PV, 256:512]).then_inc(S["dv_inv"], 1)
                dve.wait_ge(S["dv_inv"], 2 * g + quad + 1)
                for j in range(4):
                    for p in range(4):
                        w = 4 * quad + p
                        ins = dve.tensor_tensor(attended[32 * j:32 * j + 32, w * T:(w + 1) * T],
                                                psum[32 * p:32 * p + 32, PV, j * T:(j + 1) * T],
                                                inv_sum[32 * p:32 * p + 32, j * T:(j + 1) * T], ALU.mult)
                ins.then_inc(S["dv_att"], 1)

            def add_residual(c):
                dve.wait_ge(S["ac_proj"], c + 1)
                for s in range(2):
                    o = x1[:, bass.ds(c * G + s * 256, 256)].rearrange("p (w a b) -> p w a b", a=WS, b=WS)
                    ins = dve.tensor_tensor(o, stripe(projected, s), x_view(c, s), ALU.add)
                ins.then_inc(S["dv_x1"], 1)

            def normalise2(c):
                dve.wait_ge(S["ac_rstd2"], c + 1)
                dve.tensor_tensor(rstd2[:], psum[:, NORM, :], rstd2[:], ALU.mult).then_inc(S["dv_whole2"], 1)

            def add_mlp(n, par):
                dve.wait_ge(S["ac_mlp"], n + 1)
                for s in range(2):
                    o = x2[:, bass.ds(n * G + s * 256, 256)].rearrange("p (a w b) -> p w a b", a=WS, b=WS)
                    i1 = x1[:, bass.ds(n * G + s * 256, 256)].rearrange("p (w a b) -> p w a b", a=WS, b=WS)
                    dve.tensor_tensor(o, stripe(mlp_out[:, par, :], s), i1, ALU.add).then_inc(S["dv_x2"], 1)

            def high_of_normed2(c):
                dve.wait_ge(S["dv_whole2"], c + 1)
                for bh in range(2):
                    r = slice(bh * C, (bh + 1) * C)
                    ins = dve.tensor_copy(normed2[r, bh, bass.ds(c * G, G)], rstd2[r, :])
                ins.then_inc(S["dv_high2"], 1)

            def low_of_normed2(c, bh):
                dve.wait_ge(S["dv_high2"], c + 1)
                r, other = slice(bh * C, (bh + 1) * C), slice((1 - bh) * C, (2 - bh) * C)
                low_part(dve, rstd2[r, :], normed2[r, bh, bass.ds(c * G, G)], normed2[other, bh, bass.ds(c * G, G)]
                         ).then_inc(S["dv_normed2"], 1)

            def step(g, nxt, prev, older):
                if nxt is not None:
                    normalise(nxt)
                if older is not None:
                    low_of_normed2(older, 0)
                if prev is not None:
                    add_residual(prev)
                if older is not None:
                    low_of_normed2(older, 1)
                if nxt is not None:
                    k_head(nxt)
                    q_low(nxt)
                if nxt is not None:
                    take_maximum(nxt, 0)
                divide_by_sums(g, 0)
                if nxt is not None:
                    for w in range(1, 5):
                        take_maximum(nxt, w)
                if prev is not None:
                    normalise2(prev)
                if nxt is not None:
                    for w in range(5, NW):
                        take_maximum(nxt, w)
                    k_block_low(dve, nxt, 0, S["dv_kb"])
                    spread_maxima(nxt)
                divide_by_sums(g, 1)
                if prev is not None:
                    high_of_normed2(prev)

            dve.wait_ge(S["ac_sq"], 1)
            low_of_square(dve)
            split_bias()
            normalise(0)
            other_weights()
            dve.wait_ge(S["zeroed"], NBLOCKS)
            k_head(0)
            dve.wait_ge(S["ac_q"], 1)
            q_block(dve.tensor_copy, q[:])
            q_low(0)
            for bh in range(2):
                k_block_low(dve, 0, bh, S["dv_kb"])
            for w in range(NW):
                take_maximum(0, w)
            spread_maxima(0)
            step(0, 1, None, None)
            step(1, 2, 0, None)
            with dve.Fori(0, NG // 2 - 2) as i:
                step(2 * i + 2, 2 * i + 3, 2 * i + 1, 2 * i)
                step(2 * i + 3, 2 * i + 4, 2 * i + 2, 2 * i + 1)
            step(NG - 2, NG - 1, NG - 3, NG - 4)
            step(NG - 1, None, NG - 2, NG - 3)
            for bh in range(2):
                low_of_normed2(NG - 2, bh)
            add_residual(NG - 1)
            low_of_x1(dve, NG - 1)
            add_mlp(0, 0)
            low_of_square2(dve, NG - 1)
            normalise2(NG - 1)
            high_of_normed2(NG - 1)
            for bh in range(2):
                low_of_normed2(NG - 1, bh)

            def pool_image(n, b4, half):
                dve.wait_ge(S["ac_relu"], n + 1)
                dve.tensor_reduce(h_sum[:, bass.ds(n, 1)], psum[:, PW1[half], :], AX.X, ALU.add).then_inc(S["dv_hsum"], 1)
                dve.tensor_reduce(r_sum[:, bass.ds(n, 1)], relu_out[:, half, :], AX.X, ALU.add).then_inc(S["dv_rsum"], 1)

            def step_done(k, n):
                dve.wait_ge(S["gate_dve"], k * GATE_STEPS + n)

            def gate_means(k):
                mem, (b0, nb) = gates[k], GATES[k]
                dve.wait_ge(S["zeroed"], NZERO)
                dve.wait_ge(S["dv_hsum"], 2 * (b0 + nb))
                dve.wait_ge(S["dv_rsum"], 2 * (b0 + nb))
                for i, sums in enumerate((h_sum, r_sum)):
                    ins = dve.tensor_reduce(mem["pooled"][:, i, :], sums[:, 2 * b0:2 * (b0 + nb)].rearrange("p (b s) -> p b s", s=2),
                                            AX.X, ALU.add)
                ins.then_inc(S["gate_dve"], 1)
                step_done(k, 1)
                for bh in range(2):
                    r = slice(bh * C, (bh + 1) * C)
                    at = slice(2 * b0 + bh, 2 * (b0 + nb), 2)
                    dve.tensor_scalar(gaps[r, 1, at], mem["pooled"][r, 1, :], 1.0 / PIX, None, ALU.mult)
                    ins = dve.tensor_scalar(gaps[r, 0, at], mem["pooled"][r, 0, :], 1.0 / PIX, vec[r, 9:10], ALU.mult, ALU.add)
                ins.then_inc(S["gate_dve"], 1)
                step_done(k, 2)
                full = [128, 2 * nb, 6]
                dve.tensor_tensor(mem["off_products"], gaps[:, 1, 2 * b0:2 * (b0 + nb)].unsqueeze(2).to_broadcast(full),
                                  off_w.unsqueeze(1).to_broadcast(full), ALU.mult).then_inc(S["gate_dve"], 1)

            def gate_hidden(k):
                mem, n = gates[k], 2 * GATES[k][1]
                dve.wait_ge(S["gate_pe"], k * GATE_PE + 1)
                dve.tensor_scalar(mem["fc1_out"], psum[:, GATE, 0:n], vec[:, 13:14], 0.0, ALU.add, ALU.max).then_inc(S["gate_dve"], 1)

            def gate_scores(k):
                mem, n = gates[k], 2 * GATES[k][1]
                row = mem["score_row"][0:n]
                dve.wait_ge(S["gate_pe"], k * GATE_PE + 2)
                dve.tensor_tensor(row, psum[0:n, GATE, 64:64 + C], fc2_bias[0:n], ALU.add).then_inc(S["gate_dve"], 1)
                dve.tensor_tensor(mem["offset"], psum[:, GATE, 8:8 + 6 * n].rearrange("p (b t) -> p b t", t=6),
                                  off_bias.unsqueeze(1).to_broadcast([128, n, 6]), ALU.add).then_inc(S["gate_dve"], 1)

            def gate_spread(k):
                mem, n = gates[k], 2 * GATES[k][1]
                row = mem["score_row"][0:n]
                a = _AT["batch_of_row"][0]
                dve.wait_ge(S["gate_act"], k * GATE_ACT + 1)
                dve.tensor_copy(mem["score_rep"][0:n], row[:, 0:KS].unsqueeze(1).to_broadcast([n, SHIFTS, KS])).then_inc(S["gate_dve"], 1)
                dve.tensor_tensor(mem["diag"][0:n], row.unsqueeze(1).to_broadcast([n, n, C]),
                                  consts[0:n, a:a + n].unsqueeze(2).to_broadcast([n, n, C]), ALU.mult).then_inc(S["gate_dve"], 1)

            def gate_mask(k):
                mem, n = gates[k], 2 * GATES[k][1]
                greater, equal = mem["greater"], mem["equal"]
                dve.wait_ge(S["gate_pe"], k * GATE_PE + 3)
                dve.tensor_copy(mem["score_col"], psum[:, GATE, 0:n]).then_inc(S["gate_dve"], 1)
                step_done(k, 9)
                col = mem["score_col"].unsqueeze(2).to_broadcast([128, n, C])
                every = psum[:, GATE, 128:128 + n * C].rearrange("p (b c) -> p b c", c=C)
                dve.tensor_tensor(equal, every, col, ALU.is_equal).then_inc(S["gate_dve"], 1)
                dve.tensor_tensor(greater, every, col, ALU.is_gt)
                step_done(k, 10)
                dve.tensor_tensor(equal, equal, const("earlier").unsqueeze(1).to_broadcast([128, n, C]), ALU.mult).then_inc(S["gate_dve"], 1)
                step_done(k, 11)
                dve.tensor_tensor(greater, greater, equal, ALU.add).then_inc(S["gate_dve"], 1)
                step_done(k, 12)
                dve.tensor_reduce(mem["rank"], greater, AX.X, ALU.add).then_inc(S["gate_dve"], 1)
                step_done(k, 13)
                dve.tensor_scalar(mem["rank"], mem["rank"], float(KS), None, ALU.is_lt).then_inc(S["gate_dve"], 1)

            def gate_taps(k):
                mem, n = gates[k], 2 * GATES[k][1]
                mine = tap_w[:, :, 2 * GATES[k][0]:2 * GATES[k][0] + n, :]
                dve.wait_ge(S["gate_act"], k * GATE_ACT + 4)
                dve.tensor_scalar(mem["gain"], mem["gain"], 1.0, None, ALU.add).then_inc(S["gate_dve"], 1)
                step_done(k, 15)
                full = [128, 3, n, NTAP]
                by_kernel = lambda v, i: v.rearrange("p b (m two) -> p m b two", two=2)[:, :, :, i:i + 1].to_broadcast(full)
                dve.tensor_tensor(mine, taps.unsqueeze(2).to_broadcast(full), by_kernel(mem["gain"], 0), ALU.mult
                                  ).then_inc(S["gate_dve"], 1)
                dve.tensor_tensor(mem["live"], const("valid").rearrange("p (m t) -> p m t", t=NTAP).unsqueeze(2).to_broadcast(full),
                                  mem["rank"].unsqueeze(1).unsqueeze(3).to_broadcast(full), ALU.mult).then_inc(S["gate_dve"], 1)
                step_done(k, 16)
                dve.tensor_tensor(mine, mine, by_kernel(mem["shift"], 1), ALU.add).then_inc(S["gate_dve"], 1)
                step_done(k, 18)
                dve.tensor_tensor(mine, mine, mem["live"], ALU.mult).then_inc(S["gate_dve"], 1)
                step_done(k, 19)

            def product_of_5(b4, bh):
                dve.tensor_tensor(product5[:], *factors(b4, bh, 1), ALU.mult).then_inc(S["dv_product"], 1)

            def whole_weights(b4, bh):
                u = 2 * b4 + bh
                if not (isinstance(b4, int) and u == 0):
                    product_of_5(b4, bh)
                dve.wait_ge(S["po_product"], 2 * u + 1)
                dve.wait_ge(S["dv_product"], 2 * u + 1)
                window = taps_window(whole_w[:, bh], 1)
                dve.tensor_tensor(window, window, product5[:], ALU.add).then_inc(S["dv_product"], 1)
                dve.wait_ge(S["po_product"], 2 * u + 2)
                dve.wait_ge(S["dv_product"], 2 * u + 2)
                window = taps_window(whole_w[:, bh], 0)
                dve.tensor_tensor(window, window, product3[:], ALU.add).then_inc(S["dv_whole"], 1)

            def low_weights(b4, bh):
                if b4 == 0 and bh == 0:
                    dve.wait_ge(S["ac_first_high"], 1)
                    low_part(dve, whole_w[:, 0, 0:TAP], conv_w[0][:, 0, 0:TAP], conv_w[0][:, 1, 0:TAP]).then_inc(S["first_low_weights"], 1)
                    dve.wait_ge(S["ac_high"], 1)
                    low_part(dve, whole_w[:, 0, TAP:], conv_w[0][:, 0, TAP:], conv_w[0][:, 1, TAP:]).then_inc(S["low_weights"], 1)
                    return
                dve.wait_ge(S["ac_high"], 2 * b4 + bh + 1)
                dve.tensor_tensor(conv_w[bh][:, 1], whole_w[:, bh], conv_w[bh][:, 0].bitcast(F32), ALU.subtract
                                  ).then_inc(S["low_weights"], 1)

            def result(b4, bh):
                dve.wait_ge(S["pe_conv"], 2 * b4 + bh + 1)
                r = slice(bh * C, (bh + 1) * C)
                image = x2[r, bass.ds(b4 * PIX, PIX)].rearrange("p (y two x) -> p y two x", two=2, x=W)
                for parity in range(2):
                    rows = image[:, :, parity, :]
                    made = psum[parity * C:(parity + 1) * C, CONV0 + bh, :].rearrange("p (y x) -> p y x", x=W)
                    ins = dve.scalar_tensor_tensor(rows, made, vec[parity * C:(parity + 1) * C, 10:11], rows, ALU.add, ALU.add)
                ins.then_inc(S["dv_result"], 1)

            with dve.Fori(0, NG // 2 - 2) as i:
                add_mlp(2 * i + 1, 1)
                pool_image(2 * i, i, 0)
                add_mlp(2 * i + 2, 0)
                pool_image(2 * i + 1, i, 1)
            gate_means(0)
            gate_hidden(0)
            gate_scores(0)
            gate_spread(0)
            add_mlp(NG - 3, 1)
            gate_mask(0)
            gate_taps(0)
            pool_image(NG - 4, NB4 - 2, 0)
            add_mlp(NG - 2, 0)
            product_of_5(0, 0)
            pool_image(NG - 3, NB4 - 2, 1)
            add_mlp(NG - 1, 1)
            whole_weights(0, 0)
            low_weights(0, 0)
            whole_weights(0, 1)
            pool_image(NG - 2, NB4 - 1, 0)
            pool_image(NG - 1, NB4 - 1, 1)
            gate_means(1)
            gate_hidden(1)
            gate_scores(1)
            gate_spread(1)
            whole_weights(1, 0)
            result(0, 0)
            gate_mask(1)
            gate_taps(1)
            whole_weights(1, 1)
            result(0, 1)
            for b4 in range(2, NB4):
                for bh in range(2):
                    whole_weights(b4, bh)
                    result(b4 - 1, bh)
                    low_weights(b4, bh)
            result(NB4 - 1, 0)
            result(NB4 - 1, 1)


def _pack(sizes, parts):
    at, n = _columns(sizes)
    packed = np.zeros((128, n), np.float32)
    for name, blocks in parts.items():
        for row, column, v in blocks:
            v = v.reshape(len(v), -1)
            packed[row:row + v.shape[0], at[name][0] + column:at[name][0] + column + v.shape[1]] = v
    return packed


def _layout(inputs):
    a = {k: np.asarray(v) for k, v in inputs.items()}
    L0, L1 = "L0_conv_", "L1_conv_"
    kernels = []
    for k in KERNELS:
        o = (TAP - k) // 2
        w = np.pad(a[f"{L1}dw{k}"][:KS, 0], ((0, 0), (o + 1, o + 1), (o, o)))
        w = np.stack([w[:, 1:], w[:, :-1]], axis=-1)
        kernels.append(w.reshape(KS, NKT // TAP, SHIFTS, TAP, 2).transpose(2, 0, 1, 3, 4).reshape(128, NTAP))
    w_qkv, w_proj, w_mlp1 = a[L0 + "w_qkv"].reshape(C, 3, C), a[L0 + "w_proj"], a[L0 + "w_mlp1"]
    halves = (0, C)
    proj_rows = [(j * 32 + hh * 16 + bh * HD, bh * C, w_proj[(4 * hh + j) * HD:(4 * hh + j + 1) * HD])
                 for j in range(4) for hh in range(2) for bh in range(2)]
    vectors = [L0 + "ln1_scale", L0 + "ln1_bias", L0 + "ln2_scale", L0 + "ln2_bias", L0 + "b_qkv", L0 + "b_proj",
               L0 + "b_mlp2", L1 + "pw1_b", L1 + "pw_b"]
    by_channel = np.concatenate([a[v].reshape(-1, C).T for v in vectors], axis=1)
    vec = [(r, 0, by_channel) for r in halves] + [(0, 11, a[L0 + "b_mlp1"].reshape(2, 128).T), (0, 13, a[L1 + "fc1_b"].reshape(128, 1))]
    table = a[L0 + "rel_bias_table"]
    return {
        "x": a["x"].reshape(B, C, PIX),
        "consts": _constants(),
        "weights": _pack(_WEIGHTS, {
            "vec": vec,
            "proj_w": proj_rows,
            "mlp2_w": [(0, 0, a[L0 + "w_mlp2"].reshape(2, 128, C).transpose(1, 0, 2))],
            "pw1_w": [(r, r, a[L1 + "pw1_w"].T) for r in halves],
            "fc1_w": [(r, 0, a[L1 + "fc1_w"].T) for r in halves],
            "fc2_w": [(0, 0, a[L1 + "fc2_w"].T)],
            "off_w": [(r, 0, a[L1 + "off_w"].T) for r in halves],
            "off_bias": [(0, 0, np.broadcast_to(a[L1 + "off_b"], (128, 6)))],
            "fc2_bias": [(0, 0, np.broadcast_to(a[L1 + "fc2_b"], (B, C)))],
            "fuse_w": [(r * KS, 0, a[L1 + "pw_w"][:, :3 * KS].reshape(C, 3, KS).transpose(2, 1, 0)) for r in range(SHIFTS)],
            "taps": [(0, 0, np.stack(kernels, axis=1))],
        }),
        "raw": _pack(_RAW, {
            "qkv": [(r, i * 128 + r, w_qkv[:, i]) for r in halves for i in range(3)],
            "proj": [(r, r, w_proj) for r in halves],
            "mlp1": [(r, 0, w_mlp1) for r in halves],
        }),
        "rel_flipped": table[::-1], "rel_table": table,
    }


def kernel(**inputs):
    import concourse.bacc as _bacc
    from concourse.bass_utils import run_bass_kernel_spmd as _run

    nc = _bacc.Bacc("TRN2", target_bir_lowering=False, num_devices=1)
    arrays, args = {}, {}
    for name, v in _layout(inputs).items():
        v = np.ascontiguousarray(v)
        arrays[f"in_{name}"] = v
        args[name] = nc.dram_tensor(f"in_{name}", v.shape, mybir.dt.from_np(v.dtype), kind="ExternalInput").ap()
    out = nc.dram_tensor("out", (B, C, PIX), mybir.dt.float32, kind="ExternalOutput").ap()
    conv_seq_kernel(nc, args, out)
    r = _run(nc, [arrays], core_ids=[0])
    return r.results[0]["out"].reshape(B, C, H, W)
```
